# Optimizing a Trainium2 kernel written in Bass

```python
import numpy as np
import jax
import jax.numpy as jnp

def _softmax(x, axis=-1):
    return jax.nn.softmax(x, axis=axis)

def _gelu(x):
    return jax.nn.gelu(x, approximate=True)

def _silu(x):
    return jax.nn.silu(x)

def _sigmoid(x):
    return jax.nn.sigmoid(x)

def _layernorm(x, axis=-1, eps=1e-05):
    m = jnp.mean(x, axis=axis, keepdims=True)
    v = jnp.var(x, axis=axis, keepdims=True)
    return (x - m) / jnp.sqrt(v + eps)

def _scatter_add(tgt, idx, src, axis=0):
    return tgt.at[idx].add(src)

def _segment_sum(src, seg, n):
    return jax.ops.segment_sum(src, seg, n)
kernel_name = 'mk_gnn_resnorm_d4_gnn_r64_7ea764'

def setup_inputs(seed: int=0):
    np.random.seed(seed)
    _w = jnp.asarray

    def _rec_inputs():
        import jax
        import jax.numpy as jnp
        _gk = jax.random.key(seed)
        x = -0.0001006 + 1 * jax.random.normal(jax.random.fold_in(_gk, 1), (50000, 96), jnp.float32)
        src = jax.random.randint(jax.random.fold_in(_gk, 2), (25000,), 0, 50000, jnp.int32)
        dst = jax.random.randint(jax.random.fold_in(_gk, 3), (25000,), 0, 50000, jnp.int32)
        _o = jnp.argsort(dst, stable=True)
        src = src[_o]
        dst = dst[_o]
        edge_attr_17 = jax.random.uniform(jax.random.fold_in(_gk, 11), (25000, 17), jnp.float32, 0.0, 1)
        return (x, src, dst, edge_attr_17)
    x, src, dst, edge_attr_17 = _rec_inputs()

    def _L0_gnn_setup():
        import jax, jax.numpy as jnp
        import numpy as np
        N = 50000
        E = 12500
        D = 96
        ED = 17
        key = jax.random.key(seed)
        ks = jax.random.split(key, 12)
        x = jax.random.normal(ks[0], (N, D), dtype=jnp.float32)
        edge_index = jax.random.randint(ks[1], (2, E), 0, N, dtype=jnp.int64)
        edge_attr = jax.random.uniform(ks[2], (E, ED), dtype=jnp.float32)
        s = 1.0 / np.sqrt(ED)
        W1 = jax.random.uniform(ks[3], (D, ED), jnp.float32, -s, s)
        b1 = jax.random.uniform(ks[4], (D,), jnp.float32, -s, s)
        s = 1.0 / np.sqrt(D)
        W2 = jax.random.uniform(ks[5], (D, D), jnp.float32, -s, s)
        b2 = jax.random.uniform(ks[6], (D,), jnp.float32, -s, s)
        Ws = jax.random.uniform(ks[7], (D, D), jnp.float32, -s, s)
        bs = jax.random.uniform(ks[8], (D,), jnp.float32, -s, s)
        Wn = jax.random.uniform(ks[9], (D, D), jnp.float32, -s, s)
        bn = jax.random.uniform(ks[10], (D,), jnp.float32, -s, s)
        return {'x': x, 'edge_index': edge_index, 'edge_attr': edge_attr, 'W1': W1, 'b1': b1, 'W2': W2, 'b2': b2, 'Ws': Ws, 'bs': bs, 'Wn': Wn, 'bn': bn}
    _L0_gnn_all = _L0_gnn_setup()
    _L0_gnn_in = {k: v for k, v in _L0_gnn_all.items() if k in ('W1', 'b1', 'W2', 'b2', 'Ws', 'bs', 'Wn', 'bn')}
    del _L0_gnn_all

    def _L1_gnn_setup():
        import jax, jax.numpy as jnp
        import numpy as np
        K = 10
        ALPHA = 0.1
        BETA = 0.9
        N_NODES = 50000
        N_EDGES = 12500
        D_FEAT = 96
        key = jax.random.key(seed)
        k1, k2, k3 = jax.random.split(key, 3)
        x = jax.random.normal(k1, (N_NODES, D_FEAT), dtype=jnp.float32)
        row = jax.random.randint(k2, (N_EDGES,), 0, N_NODES, dtype=jnp.int64)
        col = jax.random.randint(k3, (N_EDGES,), 0, N_NODES, dtype=jnp.int64)
        edge_index = jnp.stack([row, col], axis=0)
        return {'x': x, 'edge_index': edge_index}
    _L1_gnn_all = _L1_gnn_setup()
    _L1_gnn_in = {k: v for k, v in _L1_gnn_all.items() if k in ()}
    del _L1_gnn_all

    def _L2_gnn_setup():
        import jax, jax.numpy as jnp
        import numpy as np
        K = 16
        ALPHA = 0.1
        key = jax.random.key(seed)
        k1, k2 = jax.random.split(key)
        N, E, D = (50000, 12500, 96)
        x = jax.random.normal(k1, (N, D), dtype=jnp.float32)
        edge_index = jax.random.randint(k2, (2, E), 0, N, dtype=jnp.int64)
        return {'x': x, 'edge_index': edge_index}
    _L2_gnn_all = _L2_gnn_setup()
    _L2_gnn_in = {k: v for k, v in _L2_gnn_all.items() if k in ()}
    del _L2_gnn_all

    def _L3_gnn_setup():
        import jax, jax.numpy as jnp
        import numpy as np
        N_NODES = 50000

        def gcn_conv(x, src, dst, W, b):
            n = x.shape[0]
            ew = jnp.ones(src.shape[0], dtype=x.dtype)
            deg = jax.ops.segment_sum(ew, dst, num_segments=n)
            dinv = jnp.where(deg > 0, jax.lax.rsqrt(deg), 0.0).astype(x.dtype)
            norm = dinv[src] * dinv[dst]
            xw = x @ W
            msg = xw[src] * norm[:, None]
            out = jax.ops.segment_sum(msg, dst, num_segments=n)
            return out + b

        def prelu(x, a):
            return jnp.where(x > 0, x, a * x)
        key = jax.random.key(seed)
        k1, k2, k3, k4 = jax.random.split(key, 4)
        in_dim = z_dim = 96
        n_edges = 12500
        x = jax.random.normal(k1, (N_NODES, in_dim), dtype=jnp.float32)
        edge_index = jax.random.randint(k2, (2, n_edges), 0, N_NODES, dtype=jnp.int32)
        s1 = 1.0 / np.sqrt(in_dim)
        W1 = jax.random.uniform(k3, (in_dim, z_dim), jnp.float32, -s1, s1)
        W2 = jax.random.uniform(k4, (z_dim, z_dim), jnp.float32, -s1, s1)
        b1 = jnp.zeros((z_dim,), jnp.float32)
        b2 = jnp.zeros((z_dim,), jnp.float32)
        prelu_a = jnp.full((z_dim,), 0.25, jnp.float32)
        return {'x': x, 'edge_index': edge_index, 'W1': W1, 'b1': b1, 'W2': W2, 'b2': b2, 'prelu_a': prelu_a}
    _L3_gnn_all = _L3_gnn_setup()
    _L3_gnn_in = {k: v for k, v in _L3_gnn_all.items() if k in ('W1', 'b1', 'W2', 'b2', 'prelu_a')}
    del _L3_gnn_all
    return {'x': x, 'src': src, 'dst': dst, 'edge_attr_17': edge_attr_17, 'L0_gnn_W1': _L0_gnn_in['W1'], 'L0_gnn_b1': _L0_gnn_in['b1'], 'L0_gnn_W2': _L0_gnn_in['W2'], 'L0_gnn_b2': _L0_gnn_in['b2'], 'L0_gnn_Ws': _L0_gnn_in['Ws'], 'L0_gnn_bs': _L0_gnn_in['bs'], 'L0_gnn_Wn': _L0_gnn_in['Wn'], 'L0_gnn_bn': _L0_gnn_in['bn'], 'L3_gnn_W1': _L3_gnn_in['W1'], 'L3_gnn_b1': _L3_gnn_in['b1'], 'L3_gnn_W2': _L3_gnn_in['W2'], 'L3_gnn_b2': _L3_gnn_in['b2'], 'L3_gnn_prelu_a': _L3_gnn_in['prelu_a']}

def reference(x, src, dst, edge_attr_17, L0_gnn_W1, L0_gnn_b1, L0_gnn_W2, L0_gnn_b2, L0_gnn_Ws, L0_gnn_bs, L0_gnn_Wn, L0_gnn_bn, L3_gnn_W1, L3_gnn_b1, L3_gnn_W2, L3_gnn_b2, L3_gnn_prelu_a):
    import jax
    import jax.numpy as jnp

    def _L0_gnn_ref(x, edge_index, edge_attr, W1, b1, W2, b2, Ws, bs, Wn, bn):
        import jax, jax.numpy as jnp
        import numpy as np
        N = 50000
        E = 12500
        D = 96
        ED = 17
        src, dst = (edge_index[0], edge_index[1])
        h = jax.nn.relu(edge_attr @ W1.T + b1)
        w = h @ W2.T + b2
        msg = w * x[src]
        agg = jax.ops.segment_sum(msg, dst, num_segments=x.shape[0])
        return jax.nn.relu(x @ Ws.T + bs + agg @ Wn.T + bn)

    def _L1_gnn_ref(x, edge_index):
        import jax, jax.numpy as jnp
        import numpy as np
        K = 10
        ALPHA = 0.1
        BETA = 0.9
        N_NODES = 50000
        N_EDGES = 12500
        D_FEAT = 96
        n = x.shape[0]
        row, col = (edge_index[0], edge_index[1])
        ones = jnp.ones((edge_index.shape[1],), dtype=x.dtype)
        deg_row = jnp.maximum(jax.ops.segment_sum(ones, row, num_segments=n), 1.0)
        deg_col = jnp.maximum(jax.ops.segment_sum(ones, col, num_segments=n), 1.0)
        w = jax.lax.rsqrt(deg_row[row] * deg_col[col])

        def spmm(feat):
            msg = feat[col] * w[:, None]
            return jax.ops.segment_sum(msg, row, num_segments=n)
        h = x
        out = h
        for _ in range(K):
            out = spmm(out) * BETA + h * ALPHA
        theta = BETA ** K + ALPHA * sum((BETA ** i for i in range(K)))
        return out / jnp.asarray(theta, dtype=x.dtype)

    def _L2_gnn_ref(x, edge_index):
        import jax, jax.numpy as jnp
        import numpy as np
        K = 16
        ALPHA = 0.1
        N = x.shape[0]
        loop = jnp.arange(N, dtype=edge_index.dtype)
        row = jnp.concatenate([edge_index[0], loop])
        col = jnp.concatenate([edge_index[1], loop])
        deg = jax.ops.segment_sum(jnp.ones_like(col, dtype=x.dtype), col, num_segments=N)
        deg_inv_sqrt = jnp.where(deg > 0, jax.lax.rsqrt(jnp.maximum(deg, 1e-30)), 0.0)
        norm = (deg_inv_sqrt[row] * deg_inv_sqrt[col])[:, None]
        h = x
        for _ in range(K):
            h_neighbors = jax.ops.segment_sum(norm * h[row], col, num_segments=N)
            h = (1.0 - ALPHA) * h_neighbors + ALPHA * x
        return h

    def _L3_gnn_ref(x, edge_index, W1, b1, W2, b2, prelu_a):
        import jax, jax.numpy as jnp
        import numpy as np
        N_NODES = 50000

        def gcn_conv(x, src, dst, W, b):
            n = x.shape[0]
            ew = jnp.ones(src.shape[0], dtype=x.dtype)
            deg = jax.ops.segment_sum(ew, dst, num_segments=n)
            dinv = jnp.where(deg > 0, jax.lax.rsqrt(deg), 0.0).astype(x.dtype)
            norm = dinv[src] * dinv[dst]
            xw = x @ W
            msg = xw[src] * norm[:, None]
            out = jax.ops.segment_sum(msg, dst, num_segments=n)
            return out + b

        def prelu(x, a):
            return jnp.where(x > 0, x, a * x)
        n = x.shape[0]
        loop = jnp.arange(n, dtype=edge_index.dtype)
        src = jnp.concatenate([edge_index[0], loop])
        dst = jnp.concatenate([edge_index[1], loop])
        h = prelu(gcn_conv(x, src, dst, W1, b1), prelu_a)
        h = prelu(gcn_conv(h, src, dst, W2, b2), prelu_a)
        return h
    edge_index = jnp.stack([src, dst])
    x = _layernorm(x + _L0_gnn_ref(x, edge_index, edge_attr_17, L0_gnn_W1, L0_gnn_b1, L0_gnn_W2, L0_gnn_b2, L0_gnn_Ws, L0_gnn_bs, L0_gnn_Wn, L0_gnn_bn), axis=-1)
    x = _layernorm(x + _L1_gnn_ref(x, edge_index), axis=-1)
    x = _layernorm(x + _L2_gnn_ref(x, edge_index), axis=-1)
    x = _layernorm(x + _L3_gnn_ref(x, edge_index, L3_gnn_W1, L3_gnn_b1, L3_gnn_W2, L3_gnn_b2, L3_gnn_prelu_a), axis=-1)
    return x

_drawn_inputs = setup_inputs


def setup_inputs(seed=0):
    import zlib

    import numpy as np

    out = dict(_drawn_inputs(seed))
    spreads = {'L3_gnn_b1': (0.0, 0.1), 'L3_gnn_b2': (0.0, 0.1), 'L3_gnn_prelu_a': (0.25, 0.6)}
    factors = {'edge_attr_17': 4.752, 'L0_gnn_b1': 5.387, 'L0_gnn_b2': 4.652}
    for name, (base, spread) in spreads.items():
        noise = np.random.default_rng([zlib.crc32(name.encode()), seed]).standard_normal(out[name].shape)
        drawn = base * np.exp(spread * noise) if base else spread * noise
        out[name] = jnp.asarray(drawn.astype(out[name].dtype))
    for name, factor in factors.items():
        out[name] = (out[name] * factor).astype(out[name].dtype)
    return out
```

```python
from contextlib import ExitStack

import concourse.bass as bass
import numpy as np
from concourse import mybir

fp32 = mybir.dt.float32
bf16 = mybir.dt.bfloat16
i32 = mybir.dt.int32
ALU = mybir.AluOpType
ACT = mybir.ActivationFunctionType
AXX = mybir.AxisListType.X

N, E, D, ED = 50000, 25000, 96, 17
P = 128
EP = P - 1
U = 8
H = U // 2
NI = -(-(-(-E // EP)) // U)
NT = NI * U
CH = NT // 2
FULL = E // EP
REST = E - FULL * EP
PAD = 65000.0
BIG = 1 << 20
TROWS = P * NT
LO = 256
HP = 98
NODES = HP * 2 * LO
MAGIC = 12582912.0
MF = 8
F_IN, F_OUT, F_DEND, F_SSTART, F_L2, F_L1 = range(6)
R_KEY, R_COL, R_W, R_L1, R_TGT = range(5)
NP_ = 125
NJ = N // NP_
J = 8
NG = NJ // J
ZROWS = LO
K1, K2 = 10, 16
BETA = 0.9
THETA = BETA ** K1 + 0.1 * sum(BETA ** i for i in range(K1))


def hold(eng, sem, value, turns):
    eng.wait_ge(sem, value)
    eng.sem_inc(turns, 1)


class Signal:

    def __init__(self, sem):
        self.sem, self.at = sem, 0


class Chain:

    def __init__(self, eng, sem):
        self.eng, self.sem, self.n = eng, sem, 0

    def __call__(self, instruction):
        self.n += 1
        instruction.then_inc(self.sem, 1)
        self.eng.wait_ge(self.sem, self.n)


class Program:

    def __init__(self, nc, ctx, ins, out):
        self.nc, self.ctx, self.i, self.out = nc, ctx, ins, out
        self.filled = [self.sem(f"slot_filled{u}") for u in range(U)]
        self.filled_at = 0
        self.turns = self.sem("turns_pool")
        self.turns_act = self.sem("turns_act")
        self.turns_dve = self.sem("turns_dve")
        self.turns_sp = self.sem("turns_sp")
        self.counters = {}

    def sem(self, name):
        return self.ctx.enter_context(self.nc.semaphore(name))

    def shared(self, name):
        if name not in self.counters:
            self.counters[name] = Signal(self.sem(name))
        return self.counters[name]

    def dram(self, name, shape, dt=fp32):
        return self.nc.dram_tensor(name, shape, dt).ap()

    def build(self):
        nc, ctx = self.nc, self.ctx

        def sb(name, shape, dt=fp32):
            return ctx.enter_context(nc.sbuf_tensor(name, shape, dt))

        self.bank = [ctx.enter_context(nc.psum_tensor(f"bank{b}", [P, 512], fp32)) for b in range(8)]
        self.ident = sb("ident", [P, P])
        self.src_i = sb("src_i", [P, NT], i32)
        self.dst_i = sb("dst_i", [P, NT], i32)
        self.key_d = sb("key_d", [P, NT])
        self.ones_d = sb("ones_d", [P, NT])
        self.norm = sb("norm", [P, NT])
        self.self_c = sb("self_c", [P, NT])
        self.tgt_d = sb("tgt_d", [P, NT], i32)
        self.l2 = [sb(f"l2_{k}", [P, NT], i32) for k in range(2)]
        self.key_s = sb("key_s", [P, NT])
        self.w_s = sb("w_s", [P, NT])
        self.col_i = sb("col_i", [P, NT], i32)
        self.tgt_s = sb("tgt_s", [P, NT], i32)
        self.l1 = [sb(f"l1_{k}", [P, NT], i32) for k in range(2)]
        self.G = sb("G", [P, U * D])
        self.O = sb("O", [P, U * D])
        self.cur = sb("cur", [P, 2 * U], i32)

        self.brow_d = self.dram("brow_d", [NT, P])
        self.brow_s = self.dram("brow_s", [NT, P])
        self.srow = self.dram("srow", [NT, P])
        self.hrow = self.dram("hrow", [NT, P])
        self.meta = self.dram("meta", [NODES, MF])
        self.rec = self.dram("rec", [TROWS, MF])
        self.agg_d = self.dram("agg_d", [N, D])
        self.agg_s = self.dram("agg_s", [N, D])
        self.x1 = self.dram("x1", [N, D])
        self.tab1 = self.dram("tab1", [2 * TROWS + ZROWS, D])
        self.tab2 = self.dram("tab2", [2 * TROWS + N, D])
        self.xp = self.dram("xp", [P, NT * D])
        self.x3 = self.dram("x3", [N, D])
        self.z1 = self.dram("z1", [N, D])
        self.z2 = self.dram("z2", [N, D])
        self.dinv_n = self.dram("dinv_n", [NODES, 1])

        with ExitStack() as s:
            def tmp(name, shape, dt=fp32):
                return s.enter_context(nc.sbuf_tensor(name, shape, dt))

            self.src_f = tmp("src_f", [P, NT])
            self.load_edges()
            self.cnt = tmp("cnt", [P, NT])
            self.ms = tmp("ms", [P, NT * MF])
            self.md = tmp("md", [P, NT * MF])
            self.count_edges()
            self.gather_rows("ms", self.meta, self.src_i, MF, self.ms)
            self.gather_rows("md", self.meta, self.dst_i, MF, self.md)
            self.edge_records()
        self.load_records()
        with ExitStack() as s:
            self.rows = s.enter_context(nc.sbuf_tensor("rows_l0", [P, NT * P], fp32))
            self.T = s.enter_context(nc.sbuf_tensor("T0", [P, NT * D], fp32))
            self.load_keys(self.brow_d)
            self.edge_mlp()
            self.passes("l0", "mul")
        self.dense("d0")
        with ExitStack() as s:
            self.rows = s.enter_context(nc.sbuf_tensor("rows_l1", [P, NT * P], fp32))
            self.T = s.enter_context(nc.sbuf_tensor("T1", [P, NT * D], fp32))
            self.load_keys(self.brow_s)
            self.passes("l1", "power")
        self.dense("d1")
        with ExitStack() as s:
            self.rows = s.enter_context(nc.sbuf_tensor("rows_l2", [P, NT * P], fp32))
            with ExitStack() as s2:
                self.T = s2.enter_context(nc.sbuf_tensor("T2", [P, NT * D], fp32))
                self.load_keys(self.brow_d)
                self.gather_rows("t2", self.tab2, self.dst_i, D, self.T, self.xp)
                self.passes("l2", "smooth")
            self.dense("d2")
            self.passes("l3a", "plain", self.z1)
            self.dense("d3")
            self.passes("l3b", "plain", self.z2)
        self.dense("d4")

    def load_edges(self):
        nc, i = self.nc, self.i
        with ExitStack() as s:
            def tmp(name, shape, dt=fp32):
                return s.enter_context(nc.sbuf_tensor(name, shape, dt))

            rows = [tmp(f"rows{k}", [CH, 2, P], i32) for k in range(2)]
            rowf = [tmp(f"rowf{k}", [CH, 2, P]) for k in range(2)]
            rowb = tmp("rowb", [CH, 2, P])
            high_i = tmp("high_i", [CH, 2, P], i32)
            high = tmp("high", [CH, 2, P])
            blank, landed, made, turned, stored, chain = (self.sem(f"load_{n}") for n in
                                                           ("blank", "landed", "made", "turned", "stored", "chain"))
            identity = self.sem("load_identity")
            flat = [i["src"], i["dst"]]
            block = s.enter_context(nc.Block())

            @block.gpsimd
            def _(pool):
                nc.gpsimd.memset(self.ident[:, :], 0.0).then_inc(identity, 1)
                pool.wait_ge(identity, 1)
                nc.gpsimd.affine_select(out=self.ident[:, :], in_=self.ident[:, :], compare_op=ALU.not_equal, fill=1.0,
                                        base=0, pattern=[[-1, P]], channel_multiplier=1).then_inc(identity, 1)

            @block.sync
            def _(sp):
                sp.wait_ge(blank, 2)
                n = 0

                def load(to, of):
                    nonlocal n
                    sp.dma_start(to, of).then_inc(landed, 16)
                    n += 16

                with nc.allow_non_contiguous_dma(reason="one number of each tile"):
                    for k in range(2):
                        load(rows[k][0:CH, 0, 1:P], flat[k][0:CH * EP].rearrange("(p q) -> p q", q=EP))
                        load(rows[k][0:FULL - CH, 1, 1:P],
                             flat[k][CH * EP:FULL * EP].rearrange("(p q) -> p q", q=EP))
                        load(rows[k][FULL - CH:FULL - CH + 1, 1, 1:REST + 1],
                             flat[k][FULL * EP:E].rearrange("(p q) -> p q", p=1))
                    load(rows[1][1:CH, 0, 0:1],
                         flat[1][EP - 1:EP - 1 + (CH - 1) * EP].rearrange("(p q) -> p q", q=EP)[:, 0:1])
                    last = CH * EP - 1
                    load(rows[1][0:FULL - CH, 1, 0:1],
                         flat[1][last:last + (FULL - CH) * EP].rearrange("(p q) -> p q", q=EP)[:, 0:1])
                    load(rows[1][FULL - CH:FULL - CH + 1, 1, 0:1],
                         flat[1][FULL * EP - 1:FULL * EP].rearrange("(p q) -> p q", p=1))
                self.landed_edges = n
                sp.wait_ge(made, 1)
                for k, (to, of) in enumerate(((self.brow_d, rowb), (self.srow, rowf[0]), (self.hrow, high))):
                    sp.dma_start(to.rearrange("(c p) q -> p c q", c=2), of[:, :, :]).then_inc(stored, 16)
                sp.wait_ge(stored, 48)

            @block.vector
            def _(dve):
                link = Chain(dve, chain)
                for k in range(2):
                    nc.vector.memset(rows[k][:, :, :], int(PAD)).then_inc(blank, 1)
                dve.wait_ge(landed, 16 * 9)
                for k in range(2):
                    link(nc.vector.tensor_copy(rowf[k][:, :, :], rows[k][:, :, :]))
                link(nc.vector.tensor_single_scalar(high_i[:, :, :], rows[0][:, :, :], 8, op=ALU.logical_shift_right))
                link(nc.vector.tensor_copy(rowb[:, :, :], rowf[1][:, :, :]))
                link(nc.vector.tensor_copy(rowb[:, :, 0:1], rowf[1][:, :, P - 1:P]))
                nc.vector.tensor_copy(high[:, :, :], high_i[:, :, :]).then_inc(made, 1)
                dve.wait_ge(turned, 4)
                for k, to in enumerate((self.src_f, self.key_d)):
                    for c in range(2):
                        link(nc.vector.tensor_copy(to[:, c * CH:(c + 1) * CH], self.bank[2 * k + c][:, 0:CH]))
                for to, of in ((self.src_i, self.src_f), (self.dst_i, self.key_d)):
                    link(nc.vector.tensor_single_scalar(to[:, :], of[:, :], float(N - 1), op=ALU.min))

            @block.tensor
            def _(pe):
                pe.wait_ge(identity, 2)
                pe.wait_ge(made, 1)
                for k in range(2):
                    for c in range(2):
                        nc.tensor.transpose(self.bank[2 * k + c][:, 0:CH], rowf[k][:, c, :],
                                            self.ident[0:CH, 0:CH]).then_inc(turned, 1)

    def count_edges(self):
        nc = self.nc
        with ExitStack() as s:
            def tmp(name, shape, dt=fp32):
                return s.enter_context(nc.sbuf_tensor(name, shape, dt))

            dig_i = tmp("dig_i", [P, NT], i32)
            dig_t = tmp("dig_t", [P, NT], i32)
            hi, lo = [tmp(f"hi{k}", [P, NT]) for k in range(2)], [tmp(f"lo{k}", [P, NT]) for k in range(2)]
            iota_hi = tmp("iota_hi", [P, 2 * HP], bf16)
            iota_lo = tmp("iota_lo", [P, LO], bf16)
            iota_p = tmp("iota_p", [HP, 2])
            earlier = tmp("earlier", [P, P])
            zeros = tmp("zeros", [P, 2 * LO], bf16)
            hb = tmp("hb", [HP, 2, U * P])
            sbr = tmp("sbr", [P, 2, U * P])
            oht = tmp("oht", [HP, 2, U * P])
            oh = [[tmp(f"oh{k}{u}", [P, 2 * HP], bf16) for u in range(2)] for k in range(2)]
            ol = [[tmp(f"ol{k}{u}", [P, LO], bf16) for u in range(2)] for k in range(2)]
            junk = tmp("junk", [P, LO])
            snap = [tmp(f"snap{u}", [HP, 2 * LO]) for u in range(2)]
            near, far = tmp("near", [P, NT]), tmp("far", [P, NT])
            hist = [self.bank[0][0:HP, :], self.bank[1][0:HP, :]]
            look = [self.bank[2][:, 0:LO], self.bank[3][:, 0:LO]]
            ZC = 16
            zero = tmp("zero", [P, NJ // ZC * D])
            blank, cleared = self.sem("count_blank"), self.sem("count_cleared")
            names = ("const", "rows0", "rows1", "onehot", "oht", "zeroed", "product", "snapped", "looked", "summed",
                     "chain", "pairs")
            const, rows0, rows1, onehot, ohts, zeroed, product, snapped, looked, summed, chain, pairs = (
                self.sem(f"count_{n}") for n in names)
            rows_in = (rows0, rows1)
            block = s.enter_context(nc.Block())

            @block.gpsimd
            def _(pool):
                nc.gpsimd.iota(iota_hi[:, :], pattern=[[1, 2], [2, HP]], base=0, channel_multiplier=0,
                               allow_small_or_imprecise_dtypes=True).then_inc(const, 1)
                nc.gpsimd.iota(iota_lo[:, :], pattern=[[1, LO]], base=0, channel_multiplier=0,
                               allow_small_or_imprecise_dtypes=True).then_inc(const, 1)
                nc.gpsimd.iota(iota_p[:, :], pattern=[[1, 2]], base=0, channel_multiplier=2,
                               allow_small_or_imprecise_dtypes=True).then_inc(const, 1)
                nc.gpsimd.memset(earlier[:, :], 1.0).then_inc(const, 1)
                pool.wait_ge(const, 4)
                nc.gpsimd.affine_select(out=earlier[:, :], in_=earlier[:, :], compare_op=ALU.is_gt, fill=0.0,
                                        base=0, pattern=[[-1, P]], channel_multiplier=1).then_inc(const, 1)
                nc.gpsimd.memset(zeros[:, :], 0.0).then_inc(const, 1)

            def steps(eng, body):
                with eng.Fori(0, NI // 2) as k:
                    body(k * 2, 0)
                    body(k * 2 + 1, 1)
                body(NI - 1, 0)

            @block.sync
            def _(sp):
                def body(n, b):
                    sp.wait_ge(pairs, n)
                    sp.dma_start(hb[:, b, :], self.hrow[bass.ds(n * U, U), :].rearrange("t q -> (t q)")
                                 .partition_broadcast(HP)).then_inc(rows_in[b], 16)
                    sp.dma_start(sbr[:, b, :], self.srow[bass.ds(n * U, U), :].rearrange("t q -> (t q)")
                                 .partition_broadcast(P)).then_inc(rows_in[b], 16)
                steps(sp, body)

            @block.vector
            def _(dve):
                link = Chain(dve, chain)
                for k, key in enumerate((self.src_f, self.key_d)):
                    link(nc.vector.tensor_copy(dig_i[:, :], key[:, :]))
                    link(nc.vector.tensor_single_scalar(dig_t[:, :], dig_i[:, :], 8, op=ALU.logical_shift_right))
                    link(nc.vector.tensor_copy(hi[k][:, :], dig_t[:, :]))
                    link(nc.vector.tensor_single_scalar(dig_t[:, :], dig_i[:, :], LO - 1, op=ALU.bitwise_and))
                    link(nc.vector.tensor_copy(lo[k][:, :], dig_t[:, :]))
                link(nc.vector.memset(hi[1][0:1, :], -1.0))
                nc.vector.memset(zero[:, :], 0.0).then_inc(blank, 1)
                dve.sem_inc(pairs, 1)
                dve.wait_ge(const, 6)

                def body(n, b):
                    dve.wait_ge(rows_in[b], (n - b) * 16 + 32)
                    dve.wait_ge(looked, n * U)
                    for c in range(2):
                        nc.vector.tensor_scalar(oht[:, c, :], hb[:, b, :], iota_p[:, c:c + 1], None,
                                                ALU.is_equal).then_inc(ohts, 1)
                    for u in range(U):
                        t = n * U + u
                        if u >= 2:
                            dve.wait_ge(product, n * U + (u - 1))
                        else:
                            dve.wait_ge(zeroed, 1)
                            dve.wait_ge(looked, n * U)
                            dve.wait_ge(product, n * U)
                        for k in range(2):
                            nc.vector.tensor_scalar(oh[k][u % 2][:, :], iota_hi[:, :], hi[k][:, bass.ds(t, 1)], None,
                                                    ALU.is_equal).then_inc(onehot, 1)
                            nc.vector.tensor_scalar(ol[k][u % 2][:, :], iota_lo[:, :], lo[k][:, bass.ds(t, 1)], None,
                                                    ALU.is_equal).then_inc(onehot, 1)
                        nc.vector.scalar_tensor_tensor(
                            out=junk[:, 0:P], in0=sbr[:, b, u * P:(u + 1) * P], scalar=self.src_f[:, bass.ds(t, 1)],
                            in1=earlier[:, :], op0=ALU.is_equal, op1=ALU.mult, accum_out=near[:, bass.ds(t, 1)]
                        ).then_inc(summed, 1)
                        dve.wait_ge(summed, t * 2 + 1)
                        dve.wait_ge(looked, t + 1)
                        nc.vector.scalar_tensor_tensor(
                            out=junk[:, :], in0=look[u % 2], scalar=1.0, in1=ol[0][u % 2][:, :], op0=ALU.mult,
                            op1=ALU.mult, accum_out=far[:, bass.ds(t, 1)]).then_inc(summed, 1)
                        dve.wait_ge(summed, t * 2 + 2)
                    dve.sem_inc(pairs, 1)
                steps(dve, body)
                nc.vector.tensor_add(self.cnt[:, :], near[:, :], far[:, :]).then_inc(chain, 1)

            @block.tensor
            def _(pe):
                pe.wait_ge(const, 6)
                for k in range(2):
                    nc.tensor.matmul(hist[k], zeros[:, 0:HP], zeros[:, :], start=True, stop=True).then_inc(zeroed, 1)

                def body(n, b):
                    pe.wait_ge(ohts, n * 2 + 2)
                    for u in range(U):
                        t = n * U + u
                        pe.wait_ge(snapped, t + 1)
                        if u >= 2:
                            pe.wait_ge(summed, n * 2 * U + 2 * (u - 1))
                        else:
                            pe.wait_ge(summed, n * 2 * U)
                        nc.tensor.matmul(look[u % 2], oht[:, 0, u * P:(u + 1) * P], snap[u % 2][:, 0:LO],
                                         start=True, stop=False)
                        nc.tensor.matmul(look[u % 2], oht[:, 1, u * P:(u + 1) * P], snap[u % 2][:, LO:2 * LO],
                                         start=False, stop=True).then_inc(looked, 1)
                        pe.wait_ge(onehot, n * 4 * U + 4 * (u + 1))
                        for k in range(2):
                            for c in range(2):
                                last = nc.tensor.matmul(hist[k][:, c * LO:(c + 1) * LO],
                                                        oh[k][u % 2][:, c * HP:(c + 1) * HP], ol[k][u % 2][:, :],
                                                        start=False, stop=True, skip_group_check=True)
                        last.then_inc(product, 1)
                steps(pe, body)

            @block.scalar
            def _(act):
                act.wait_ge(blank, 1)
                for table in (self.agg_d, self.agg_s):
                    v = table.rearrange("(c p j) d -> c p (j d)", p=NP_, j=NJ // ZC)
                    for c in range(ZC):
                        act.dma_start(v[c], zero[0:NP_, :]).then_inc(cleared, 16)
                act.dma_start(self.tab1[2 * TROWS:2 * TROWS + P, :], zero[:, 0:D]).then_inc(cleared, 16)
                act.dma_start(self.tab1[2 * TROWS + P:2 * TROWS + 2 * P, :], zero[:, 0:D]).then_inc(cleared, 16)
                for table, row in ((self.tab1, TROWS), (self.tab2, N), (self.tab2, N + TROWS)):
                    v = table[row:row + TROWS, :].rearrange("(c p j) d -> c p (j d)", p=P, j=NJ // ZC)
                    for c in range(TROWS // P // (NJ // ZC)):
                        act.dma_start(v[c], zero[:, :]).then_inc(cleared, 16)
                act.wait_ge(zeroed, 2)

                def body(n, b):
                    for u in range(U):
                        act.wait_ge(product, n * U + u)
                        if u >= 2:
                            act.wait_ge(looked, n * U + (u - 1))
                        else:
                            act.wait_ge(looked, n * U)
                        nc.scalar.activation(snap[u % 2][:, :], hist[0], ACT.Copy).then_inc(snapped, 1)
                steps(act, body)
                act.wait_ge(cleared, 16 * (2 * ZC + 2 + 3 * (TROWS // P // (NJ // ZC))))
        self.node_records()

    def node_records(self):
        nc = self.nc
        with ExitStack() as s:
            def tmp(name, shape, dt=fp32):
                return s.enter_context(nc.sbuf_tensor(name, shape, dt))

            M = 2 * LO
            deg = [tmp(f"deg{k}", [HP, M]) for k in range(2)]
            cum, end, place, t_of, mask = (tmp(n, [HP, M]) for n in ("cum", "end", "place", "t_of", "mask"))
            ones = tmp("ones", [HP, M])
            alt = [tmp("alt0", [HP, M]), tmp("alt1", [HP, M])]
            tri = tmp("tri", [HP, HP])
            off = tmp("off", [HP, 1])
            record = tmp("record", [HP, M, MF])
            dinv = tmp("dinv", [HP, M])
            const, totals, offs, chain, made, stored = (self.sem(f"node_{n}") for n in
                                                        ("const", "totals", "offs", "chain", "made", "stored"))
            block = s.enter_context(nc.Block())

            @block.gpsimd
            def _(pool):
                nc.gpsimd.memset(tri[:, :], 1.0).then_inc(const, 1)
                pool.wait_ge(const, 1)
                nc.gpsimd.affine_select(out=tri[:, :], in_=tri[:, :], compare_op=ALU.is_gt, fill=0.0, base=0,
                                        pattern=[[1, HP]], channel_multiplier=-1).then_inc(const, 1)
                nc.gpsimd.iota(alt[0][:, :], pattern=[[0, 2], [1, LO]], base=2 * TROWS, channel_multiplier=0,
                               allow_small_or_imprecise_dtypes=True).then_inc(const, 1)
                nc.gpsimd.iota(alt[1][:, :], pattern=[[1, M]], base=0, channel_multiplier=M,
                               allow_small_or_imprecise_dtypes=True).then_inc(const, 1)
                nc.gpsimd.memset(record[:, :, :], 0.0).then_inc(const, 1)

            @block.tensor
            def _(pe):
                for k in range(2):
                    pe.wait_ge(totals, k + 1)
                    nc.tensor.matmul(self.bank[2 + k][0:HP, 0:1], tri[:, :], cum[:, M - 1:M], start=True,
                                     stop=True).then_inc(offs, 1)

            @block.vector
            def _(dve):
                link = Chain(dve, chain)
                link(nc.vector.memset(ones[:, :], 1.0))
                dve.wait_ge(const, 5)
                for k in range(2):
                    link(nc.vector.tensor_copy(deg[k][:, :], self.bank[k][0:HP, :]))
                    link(nc.vector.tensor_tensor_scan(out=cum[:, :], data0=ones[:, :], data1=deg[k][:, :], initial=0.0,
                                                      op0=ALU.mult, op1=ALU.add))
                    dve.sem_inc(totals, 1)
                    dve.wait_ge(offs, k + 1)
                    link(nc.vector.tensor_copy(off[:, :], self.bank[2 + k][0:HP, 0:1]))
                    link(nc.vector.tensor_scalar(end[:, :], cum[:, :], off[:, 0:1], -1.0, ALU.add, ALU.add))
                    link(nc.vector.tensor_scalar(t_of[:, :], end[:, :], float(-(EP // 2)), 1.0 / EP, ALU.add, ALU.mult))
                    link(nc.vector.tensor_scalar(t_of[:, :], t_of[:, :], MAGIC, None, ALU.add))
                    link(nc.vector.tensor_scalar(t_of[:, :], t_of[:, :], -MAGIC, None, ALU.add))
                    link(nc.vector.tensor_scalar(place[:, :], end[:, :], 1.0, float(NT), ALU.add, ALU.mult))
                    link(nc.vector.scalar_tensor_tensor(out=place[:, :], in0=t_of[:, :], scalar=float(1 - EP * NT),
                                                        in1=place[:, :], op0=ALU.mult, op1=ALU.add))
                    link(nc.vector.tensor_single_scalar(mask[:, :], deg[k][:, :], 0.5, op=ALU.is_gt))
                    link(nc.vector.scalar_tensor_tensor(out=place[:, :], in0=place[:, :], scalar=float(N * k),
                                                        in1=alt[k][:, :], op0=ALU.add, op1=ALU.subtract))
                    link(nc.vector.tensor_mul(place[:, :], place[:, :], mask[:, :]))
                    link(nc.vector.tensor_add(record[:, :, (F_L1, F_L2)[k]], place[:, :], alt[k][:, :]))
                    link(nc.vector.tensor_copy(record[:, :, (F_OUT, F_IN)[k]], deg[k][:, :]))
                    if k == 0:
                        link(nc.vector.scalar_tensor_tensor(out=record[:, :, F_SSTART], in0=end[:, :], scalar=1.0,
                                                            in1=deg[k][:, :], op0=ALU.add, op1=ALU.subtract))
                    else:
                        link(nc.vector.tensor_copy(record[:, :, F_DEND], end[:, :]))
                link(nc.vector.tensor_scalar(dinv[:, :], deg[1][:, :], 1.0, None, ALU.add))
                link(nc.vector.reciprocal(dinv[:, :], dinv[:, :]))
                dve.sem_inc(made, 1)

            @block.sync
            def _(sp):
                sp.wait_ge(made, 1)
                sp.dma_start(self.meta.rearrange("(p m) f -> p (m f)", p=HP),
                             record[:, :, :].rearrange("p m f -> p (m f)")).then_inc(stored, 16)
                sp.dma_start(self.dinv_n.rearrange("(p m) f -> p (m f)", p=HP), dinv[:, :]).then_inc(stored, 16)
                sp.wait_ge(stored, 32)

    def gather_rows(self, name, table, index, width, to, copy=None):
        nc = self.nc
        picked, moved, stored = (self.shared(f"gather_{n}") for n in ("picked", "moved", "stored"))
        filled, at = self.filled, self.filled_at
        slot = [self.G[:, u * width:(u + 1) * width] for u in range(U)]
        with nc.Block() as block:

            @block.gpsimd
            def _(pool):
                with pool.Fori(0, NI) as n:
                    for h in range(2):
                        hold(pool, moved.sem, moved.at + n * 2 + h + 1, self.turns)
                        nc.gpsimd.tensor_copy(self.cur[:, h * H:(h + 1) * H],
                                              index[:, bass.ds(n * U + h * H, H)]).then_inc(picked.sem, 1)
                        hold(pool, picked.sem, picked.at + n * 2 + h + 1, self.turns)
                        for u in range(h * H, (h + 1) * H):
                            nc.gpsimd.indirect_dma_start(
                                out=slot[u], out_offset=None, in_=table,
                                in_offset=bass.IndirectOffsetOnAxis(ap=self.cur[:, u:u + 1], axis=0),
                            ).then_inc(filled[u], 16)

            @block.vector
            def _(dve):
                dve.sem_inc(moved.sem, 2)
                with dve.Fori(0, NI) as n:
                    for h in range(2):
                        for u in range(h * H, (h + 1) * H):
                            hold(dve, filled[u], at + n * 16 + 16, self.turns_dve)
                        nc.vector.tensor_copy(to[:, bass.ds((n * U + h * H) * width, H * width)],
                                              self.G[:, h * H * width:(h + 1) * H * width]).then_inc(moved.sem, 1)

            if copy is not None:
                @block.sync
                def _(sp):
                    sp.wait_ge(moved.sem, moved.at + 2 * NI + 2)
                    sp.dma_start(copy, to[:, :]).then_inc(stored.sem, 16)
                    sp.wait_ge(stored.sem, stored.at + 16)
        self.filled_at += 16 * NI
        picked.at += 2 * NI
        moved.at += 2 * NI + 2
        stored.at += 16 * (copy is not None)

    def edge_records(self):
        nc = self.nc
        with ExitStack() as s:
            def tmp(name, shape, dt=fp32):
                return s.enter_context(nc.sbuf_tensor(name, shape, dt))

            valid, rank, a, b, c, edge = (tmp(n, [P, NT]) for n in ("valid", "rank", "wa", "wb", "wc", "edge"))
            record, blank = tmp("edge_record", [P, NT, MF]), tmp("blank_record", [P, NT, MF])
            row = tmp("record_row", [P, NT], i32)
            ring = tmp("record_ring", [P, U * MF])
            ms = self.ms[:, :].rearrange("p (t f) -> p t f", f=MF)
            md = self.md[:, :].rearrange("p (t f) -> p t f", f=MF)
            const, roots, rooted, ready, blanked, stored, chain, picked, moved, sent0, sent1 = (
                self.sem(f"record_{n}") for n in ("const", "roots", "rooted", "ready", "blanked", "stored", "chain",
                                                  "picked", "moved", "sent0", "sent1"))
            sent = (sent0, sent1)
            block = s.enter_context(nc.Block())

            @block.scalar
            def _(act):
                act.wait_ge(roots, 1)
                for x in (a, b, c):
                    nc.scalar.activation(x[:, :], x[:, :], ACT.Sqrt).then_inc(rooted, 1)

            @block.sync
            def _(sp):
                sp.wait_ge(blanked, 1)
                sp.dma_start(self.rec.rearrange("(p t) f -> p (t f)", p=P),
                             blank[:, :, :].rearrange("p t f -> p (t f)")).then_inc(stored, 16)

            @block.vector
            def _(dve):
                v = nc.vector
                link = Chain(dve, chain)
                link(v.memset(blank[:, :, :], 0.0))
                link(v.memset(blank[:, :, R_KEY], PAD))
                link(v.memset(blank[:, :, R_L1], float(2 * TROWS)))
                link(v.memset(blank[:, :, R_TGT], float(BIG)))
                link(v.memset(record[:, :, :], 0.0))
                dve.sem_inc(blanked, 1)
                link(v.tensor_single_scalar(valid[:, :], self.src_f[:, :], float(N), op=ALU.is_lt))
                link(v.tensor_scalar(a[:, :], ms[:, :, F_IN], 1.0, None, ALU.add))
                link(v.tensor_scalar(b[:, :], md[:, :, F_IN], 1.0, None, ALU.add))
                link(v.tensor_scalar(c[:, :], ms[:, :, F_OUT], 1.0, None, ALU.max))
                link(v.tensor_scalar(rank[:, :], md[:, :, F_IN], 1.0, None, ALU.max))
                link(v.tensor_mul(c[:, :], c[:, :], rank[:, :]))
                link(v.reciprocal(self.self_c[:, :], b[:, :]))
                link(v.tensor_single_scalar(self.self_c[:, :], self.self_c[:, :], 0.9, op=ALU.mult))
                dve.sem_inc(roots, 1)
                link(v.tensor_add(rank[:, :], ms[:, :, F_SSTART], self.cnt[:, :]))
                dve.wait_ge(const, 1)
                link(v.tensor_tensor(out=edge[:, :], in0=edge[:, :], in1=md[:, :, F_DEND], op=ALU.is_equal))
                link(v.tensor_mul(edge[:, :], edge[:, :], valid[:, :]))
                link(v.scalar_tensor_tensor(out=edge[:, :], in0=self.key_d[:, :], scalar=float(-BIG), in1=edge[:, :],
                                            op0=ALU.add, op1=ALU.mult))
                link(v.tensor_scalar(self.tgt_d[:, :], edge[:, :], float(BIG), None, ALU.add))
                link(v.tensor_add(edge[:, :], ms[:, :, F_SSTART], ms[:, :, F_OUT]))
                link(v.tensor_scalar(edge[:, :], edge[:, :], -1.0, None, ALU.add))
                link(v.tensor_tensor(out=edge[:, :], in0=edge[:, :], in1=rank[:, :], op=ALU.is_equal))
                link(v.scalar_tensor_tensor(out=edge[:, :], in0=self.src_f[:, :], scalar=float(-BIG), in1=edge[:, :],
                                            op0=ALU.add, op1=ALU.mult))
                link(v.tensor_scalar(record[:, :, R_TGT], edge[:, :], float(BIG), None, ALU.add))
                link(v.tensor_copy(record[:, :, R_KEY], self.src_f[:, :]))
                link(v.tensor_copy(record[:, :, R_COL], self.key_d[:, :]))
                link(v.tensor_copy(record[:, :, R_L1], md[:, :, F_L1]))
                link(v.scalar_tensor_tensor(out=rank[:, :], in0=rank[:, :], scalar=float(1 - BIG), in1=valid[:, :],
                                            op0=ALU.add, op1=ALU.mult))
                link(v.tensor_scalar(row[:, :], rank[:, :], float(BIG), None, ALU.add))
                link(v.tensor_copy(self.l2[0][:, :], ms[:, :, F_L2]))
                link(v.tensor_single_scalar(edge[:, :], ms[:, :, F_L2], float(N), op=ALU.is_ge))
                link(v.scalar_tensor_tensor(out=self.l2[1][:, :], in0=edge[:, :], scalar=float(TROWS),
                                            in1=ms[:, :, F_L2], op0=ALU.mult, op1=ALU.add))
                dve.wait_ge(rooted, 3)
                for x in (a, b, c):
                    link(v.reciprocal(x[:, :], x[:, :]))
                link(v.tensor_mul(a[:, :], a[:, :], b[:, :]))
                link(v.tensor_mul(self.norm[:, :], a[:, :], valid[:, :]))
                link(v.scalar_tensor_tensor(out=record[:, :, R_W], in0=c[:, :], scalar=BETA, in1=valid[:, :],
                                            op0=ALU.mult, op1=ALU.mult))
                link(v.memset(self.norm[0:1, :], 1.0))
                link(v.memset(self.ones_d[:, :], 1.0))
                link(v.tensor_mul(self.ones_d[:, :], self.ones_d[:, :], valid[:, :]))
                link(v.memset(self.ones_d[0:1, :], 1.0))
                with dve.Fori(0, NI) as n:
                    for h in range(2):
                        hold(dve, sent[h], n * 16 * H, self.turns_dve)
                        nc.vector.tensor_copy(ring[:, h * H * MF:(h + 1) * H * MF].rearrange("p (t f) -> p t f", f=MF),
                                              record[:, bass.ds(n * U + h * H, H), :]).then_inc(moved, 1)

            @block.gpsimd
            def _(pool):
                nc.gpsimd.iota(edge[:, :], pattern=[[EP, NT]], base=-1, channel_multiplier=1,
                               allow_small_or_imprecise_dtypes=True).then_inc(const, 1)
                pool.wait_ge(stored, 16)
                with pool.Fori(0, NI) as n:
                    for h in range(2):
                        hold(pool, moved, n * 2 + h + 1, self.turns)
                        nc.gpsimd.tensor_copy(self.cur[:, h * H:(h + 1) * H],
                                              row[:, bass.ds(n * U + h * H, H)]).then_inc(picked, 1)
                        hold(pool, picked, n * 2 + h + 1, self.turns)
                        for u in range(h * H, (h + 1) * H):
                            nc.gpsimd.indirect_dma_start(
                                out=self.rec, out_offset=bass.IndirectOffsetOnAxis(ap=self.cur[:, u:u + 1], axis=0),
                                in_=ring[:, u * MF:(u + 1) * MF], in_offset=None, bounds_check=TROWS - 1,
                                oob_is_err=False).then_inc(sent[h], 16)
                for h in range(2):
                    pool.wait_ge(sent[h], 16 * H * NI)

    def load_records(self):
        nc = self.nc
        with ExitStack() as s:
            def tmp(name, shape, dt=fp32):
                return s.enter_context(nc.sbuf_tensor(name, shape, dt))

            got = tmp("records", [P, NT, MF])
            step = tmp("record_step", [P, NT])
            rowb = tmp("rowb_s", [CH, 2, P])
            landed, keyed, turned, made, stored, chain = (self.sem(f"order_{n}") for n in
                                                          ("landed", "keyed", "turned", "made", "stored", "chain"))
            tiles = bass.AP(self.rec.tensor, 0, [[MF, P], [EP * MF, NT], [1, MF]])
            block = s.enter_context(nc.Block())

            @block.sync
            def _(sp):
                sp.dma_start(got[:, :, :], tiles).then_inc(landed, 16)
                sp.wait_ge(made, 1)
                sp.dma_start(self.brow_s.rearrange("(c p) q -> p c q", c=2), rowb[:, :, :]).then_inc(stored, 16)
                sp.wait_ge(stored, 16)

            @block.vector
            def _(dve):
                v = nc.vector
                link = Chain(dve, chain)
                dve.wait_ge(landed, 16)
                link(v.tensor_copy(self.key_s[:, :], got[:, :, R_KEY]))
                dve.sem_inc(keyed, 1)
                link(v.tensor_copy(self.w_s[:, :], got[:, :, R_W]))
                link(v.memset(self.w_s[0:1, :], 1.0))
                link(v.tensor_copy(self.col_i[:, :], got[:, :, R_COL]))
                link(v.tensor_copy(self.tgt_s[:, :], got[:, :, R_TGT]))
                link(v.memset(self.tgt_s[0:1, :], BIG))
                link(v.tensor_copy(self.l1[0][:, :], got[:, :, R_L1]))
                link(v.tensor_single_scalar(step[:, :], got[:, :, R_L1], float(2 * TROWS), op=ALU.is_lt))
                link(v.scalar_tensor_tensor(out=self.l1[1][:, :], in0=step[:, :], scalar=float(TROWS),
                                            in1=got[:, :, R_L1], op0=ALU.mult, op1=ALU.add))
                dve.wait_ge(turned, 2)
                for c in range(2):
                    link(v.tensor_copy(rowb[:, c, :], self.bank[c][0:CH, 0:P]))
                link(v.tensor_copy(rowb[:, :, 0:1], rowb[:, :, P - 1:P]))
                dve.sem_inc(made, 1)

            @block.tensor
            def _(pe):
                pe.wait_ge(keyed, 1)
                for c in range(2):
                    nc.tensor.transpose(self.bank[c][0:CH, 0:P], self.key_s[:, c * CH:(c + 1) * CH],
                                        self.ident[:, :]).then_inc(turned, 1)

    def load_keys(self, brow):
        nc = self.nc
        landed = self.shared("keys_landed")
        with nc.Block() as block:

            @block.sync
            def _(sp):
                sp.dma_start(self.rows[:, :], brow.rearrange("t q -> (t q)").partition_broadcast(P)
                             ).then_inc(landed.sem, 16)
                sp.wait_ge(landed.sem, landed.at + 16)
        landed.at += 16

    def edge_mlp(self):
        nc, i = self.nc, self.i
        with ExitStack() as s:
            def tmp(name, shape, dt=fp32):
                return s.enter_context(nc.sbuf_tensor(name, shape, dt))

            C = ED + 1
            w1 = tmp("w1a", [C, D])
            w2 = tmp("w2a", [D + 1, D])
            ea = tmp("ea", [P, 2, U * C])
            eat = tmp("eat", [C, U * P])
            hid = tmp("hid", [D + 1, U * P])
            weights, blank, in0, in1, turned, copied, hidden, rect, product, kept = (
                self.sem(f"mlp_{n}") for n in ("weights", "blank", "in0", "in1", "turned", "copied", "hidden",
                                               "rect", "product", "kept"))
            landed = (in0, in1)
            of = i["ea"]
            block = s.enter_context(nc.Block())

            def steps(eng, body):
                with eng.Fori(0, NI // 2) as k:
                    body(k * 2, 0)
                    body(k * 2 + 1, 1)
                body(NI - 1, 0)

            @block.sync
            def _(sp):
                with nc.allow_non_contiguous_dma(reason="weights are transposed once"):
                    sp.dma_start(w1[0:ED, :], i["W1"].rearrange("c k -> k c")).then_inc(weights, 16)
                    sp.dma_start(w1[ED:C, :], i["b1"].rearrange("(a c) -> a c", a=1)).then_inc(weights, 16)
                    sp.dma_start(w2[0:D, :], i["W2"].rearrange("c k -> k c")).then_inc(weights, 16)
                    sp.dma_start(w2[D:D + 1, :], i["b2"].rearrange("(a c) -> a c", a=1)).then_inc(weights, 16)
                    sp.wait_ge(blank, 2)

                    def body(n, b):
                        v = ea[:, b, :].rearrange("p (t c) -> p t c", c=C)
                        sp.wait_ge(turned, n * 2 + 2)
                        if isinstance(n, int):
                            first = n * U * EP
                            full = (E - first) // EP
                            sp.dma_start(v[1:P, 0:full, 0:ED], of[first:first + full * EP, :].rearrange(
                                "(t q) c -> q t c", q=EP)).then_inc(landed[b], 16)
                            sp.dma_start(v[1:REST + 1, full:full + 1, 0:ED], of[first + full * EP:E, :].rearrange(
                                "(t q) c -> q t c", t=1)).then_inc(landed[b], 16)
                        else:
                            sp.dma_start(v[1:P, :, 0:ED], of[bass.ds(n * (U * EP), U * EP), :].rearrange(
                                "(t q) c -> q t c", q=EP)).then_inc(landed[b], 16)
                    steps(sp, body)

            @block.vector
            def _(dve):
                for b in range(2):
                    nc.vector.memset(ea[:, b, :], 1.0).then_inc(blank, 1)
                nc.vector.memset(hid[D:D + 1, :], 1.0).then_inc(blank, 1)

                def body(n, b):
                    for k in range(2):
                        dve.wait_ge(product, n * 2 + k + 1)
                        nc.vector.tensor_copy(self.T[:, bass.ds((n * U + k * H) * D, H * D)],
                                              self.bank[4 + k][:, 0:H * D]).then_inc(kept, 1)
                steps(dve, body)

            @block.tensor
            def _(pe):
                pe.sem_inc(turned, 4)
                pe.wait_ge(weights, 64)
                pe.wait_ge(blank, 3)

                def body(n, b):
                    pe.wait_ge(landed[b], 16 * (n // 2 + 2) if isinstance(n, int) else (n - b) * 8 + 16)
                    for k in range(2):
                        pe.wait_ge(copied, n * 2)
                        for u in range(k * H, (k + 1) * H):
                            last = nc.tensor.transpose(self.bank[k][0:C, (u - k * H) * P:(u - k * H + 1) * P],
                                                       ea[:, b, u * C:(u + 1) * C], self.ident[:, :])
                        last.then_inc(turned, 1)
                    for k in range(2):
                        pe.wait_ge(copied, n * 2 + k + 1)
                        pe.wait_ge(rect, n * 2)
                        nc.tensor.matmul(self.bank[2 + k][0:D, :], w1[:, :], eat[:, k * H * P:(k + 1) * H * P],
                                         start=True, stop=True).then_inc(hidden, 1)
                    for k in range(2):
                        pe.wait_ge(rect, n * 2 + k + 1)
                        pe.wait_ge(kept, n * 2)
                        for u in range(k * H, (k + 1) * H):
                            last = nc.tensor.matmul(self.bank[4 + k][:, (u - k * H) * D:(u - k * H + 1) * D],
                                                    hid[:, u * P:(u + 1) * P], w2[:, :], start=True, stop=True)
                        last.then_inc(product, 1)
                steps(pe, body)

            @block.scalar
            def _(act):
                def body(n, b):
                    for k in range(2):
                        act.wait_ge(turned, n * 2 + k + 5)
                        act.wait_ge(hidden, n * 2)
                        nc.scalar.activation(eat[:, k * H * P:(k + 1) * H * P], self.bank[k][0:C, :],
                                             ACT.Copy).then_inc(copied, 1)
                    for k in range(2):
                        act.wait_ge(hidden, n * 2 + k + 1)
                        act.wait_ge(product, n * 2)
                        nc.scalar.activation(hid[0:D, k * H * P:(k + 1) * H * P], self.bank[2 + k][0:D, :],
                                             ACT.Relu).then_inc(rect, 1)
                steps(act, body)

    def passes(self, name, mode, table=None):
        nc = self.nc
        K = {"mul": 1, "plain": 1, "power": K1, "smooth": K2}[mode]
        tables = {"power": self.tab1, "smooth": self.tab2}.get(mode)
        table_at = N if mode == "smooth" else 0
        first = {"mul": self.i["x"], "plain": table, "power": self.x1,
                 "smooth": self.tab2}[mode]
        index0 = self.col_i if mode == "power" else self.src_i
        later = self.l1 if mode == "power" else self.l2
        agg, target = (self.agg_s, self.tgt_s) if mode == "power" else (self.agg_d, self.tgt_d)
        key = self.key_s if mode == "power" else self.key_d
        weight = {"mul": self.ones_d, "power": self.w_s}.get(mode, self.norm)
        update = mode in ("power", "smooth")
        sig = {n: self.shared(f"pass_{n}") for n in ("picked", "placed", "multiplied", "carry_made", "carried", "gated",
                                                     "emptied", "updated0", "updated1", "linked", "ready", "scaled")}
        stored = [self.shared(f"pass_stored{h}") for h in range(2)]
        sent = [self.shared(f"pass_sent{h}") for h in range(2)]
        landed = [self.shared(f"pass_landed{h}") for h in range(2)]
        picked, placed, multiplied, carry_made, carried, gated, emptied, linked, ready, scaled = (
            sig[n] for n in ("picked", "placed", "multiplied", "carry_made", "carried", "gated", "emptied", "linked", "ready", "scaled"))
        updated = [sig["updated0"], sig["updated1"]]
        filled, at = self.filled, self.filled_at
        main, carry = self.bank[0:4], self.bank[4:6]
        O, G = self.O, self.G
        HD = H * D

        def rounds(eng, one):
            one(0, 0, True, K == 1)
            if K > 2:
                with eng.Fori(0, (K - 2) // 2) as k:
                    one(k * 2 + 1, 1, False, False)
                    one(k * 2 + 2, 0, False, False)
            if K > 1:
                one(K - 1, (K - 1) % 2, False, True)

        def at_cols(start, size):
            return slice(start, start + size) if isinstance(start, int) else bass.ds(start, size)

        with ExitStack() as s:
            def tmp(n, shape, dt=fp32):
                return s.enter_context(nc.sbuf_tensor(f"{name}_{n}", shape, dt))

            S = tmp("S", [P, U * P])
            if mode == "smooth":
                xs, x01, own = tmp("xs", [P, 2 * HD]), tmp("x01", [P, 2 * HD]), tmp("own", [P, 2 * HD])
            block = s.enter_context(nc.Block())

            @block.gpsimd
            def _(pool):
                def one(p, par, is_first, is_last):
                    source = first if is_first else tables
                    index = index0 if is_first else later[(par + 1) % 2]
                    if not is_first:
                        for h in range(2):
                            hold(pool, stored[h].sem, stored[h].at + p * 16 * NI, self.turns)

                    def pick(n, h):
                        hold(pool, multiplied.sem, multiplied.at + (p * NI + n) * U + (h * H + H), self.turns)
                        nc.gpsimd.tensor_copy(self.cur[:, h * H:(h + 1) * H],
                                              index[:, at_cols(n * U + h * H, H)]).then_inc(picked.sem, 1)

                    def gather(n, h, ends=False):
                        hold(pool, picked.sem, picked.at + (p * NI + n) * 2 + h + 1, self.turns)
                        for u in range(h * H, (h + 1) * H):
                            if u == (h + 1) * H - 1 and not ends:
                                pick(n + h, 1 - h)
                            nc.gpsimd.indirect_dma_start(
                                out=G[:, u * D:(u + 1) * D], out_offset=None, in_=source,
                                in_offset=bass.IndirectOffsetOnAxis(ap=self.cur[:, u:u + 1], axis=0),
                            ).then_inc(filled[u], 16)

                    def scatter(n, h):
                        if update:
                            hold(pool, updated[h].sem, updated[h].at + p * NI + n + 1, self.turns)
                        else:
                            hold(pool, emptied.sem, emptied.at + 4 + (p * NI + n) * U + (h * H + H), self.turns)
                        hold(pool, sent[h].sem, sent[h].at + n * 16 * H, self.turns)
                        nc.gpsimd.tensor_copy(self.cur[:, U + h * H:U + (h + 1) * H],
                                              target[:, at_cols(n * U + h * H, H)]).then_inc(placed.sem, 1)
                        hold(pool, placed.sem, placed.at + n * 2 + h + 1, self.turns)
                        for u in range(h * H, (h + 1) * H):
                            nc.gpsimd.indirect_dma_start(
                                out=agg, out_offset=bass.IndirectOffsetOnAxis(ap=self.cur[:, U + u:U + u + 1], axis=0),
                                in_=O[:, u * D:(u + 1) * D], in_offset=None, bounds_check=N - 1, oob_is_err=False,
                            ).then_inc(sent[h].sem, 16)

                    pick(0, 0)
                    if not is_last:
                        with pool.Fori(0, NI - 1) as n:
                            for h in range(2):
                                gather(n, h)
                        gather(NI - 1, 0)
                        gather(NI - 1, 1, ends=True)
                    else:
                        for h in range(2):
                            gather(0, h)
                        with pool.Fori(0, NI - 2) as n:
                            for h in range(2):
                                gather(n + 1, h)
                                scatter(n, h)
                        for h in range(2):
                            gather(NI - 1, h, ends=h == 1)
                            scatter(NI - 2, h)
                        for h in range(2):
                            scatter(NI - 1, h)
                        for h in range(2):
                            pool.wait_ge(sent[h].sem, sent[h].at + 16 * H * NI)
                rounds(pool, one)

            @block.tensor
            def _(pe):
                pe.sem_inc(multiplied.sem, U)

                def one(p, par, is_first, is_last):
                    with pe.Fori(0, NI) as n:
                        for u in range(U):
                            tile = (p * NI + n) * U + u
                            pe.wait_ge(carried.sem, carried.at + tile + 1)
                            nc.tensor.matmul(carry[u % 2][0:1, 0:D], S[:, u * P:u * P + 1],
                                             G[:, u * D:(u + 1) * D], start=True, stop=True).then_inc(carry_made.sem, 1)
                            pe.wait_ge(emptied.sem, emptied.at + tile + 1)
                            nc.tensor.matmul(main[u % 4][:, 0:D], S[:, u * P:(u + 1) * P],
                                             G[:, u * D:(u + 1) * D], start=True, stop=True).then_inc(multiplied.sem, 1)
                rounds(pe, one)

            @block.scalar
            def _(act):
                act.sem_inc(emptied.sem, 4)

                def fetch(n, h):
                    act.dma_start(xs[:, h * HD:(h + 1) * HD], self.xp[:, at_cols((n * U + h * H) * D, HD)]
                                  ).then_inc(landed[h].sem, 16)

                def one(p, par, is_first, is_last):
                    def half_of(n, h, follows):
                        step = p * NI + n
                        if update:
                            act.wait_ge(updated[h].sem, updated[h].at + step)
                            act.sem_inc(self.turns_act, 1)
                        if mode == "power" and not is_last:
                            act.wait_ge(stored[h].sem, stored[h].at + step * 16)
                            act.sem_inc(self.turns_act, 1)
                        if mode == "power" and is_last:
                            act.wait_ge(stored[h].sem, stored[h].at + (K - 1) * NI * 16)
                        if is_last:
                            act.wait_ge(sent[h].sem, sent[h].at + n * 16 * H)
                            act.sem_inc(self.turns_act, 1)
                        if mode == "smooth":
                            if is_last and not (isinstance(n, int) and n == 0):
                                fetch(n, h)
                            act.wait_ge(landed[h].sem, landed[h].at + step * 16 + 16)
                            nc.scalar.activation(x01[:, h * HD:(h + 1) * HD], xs[:, h * HD:(h + 1) * HD], ACT.Copy,
                                                 scale=0.1).then_inc(scaled.sem, 1)
                        for u in range(h * H, (h + 1) * H):
                            act.wait_ge(multiplied.sem, multiplied.at + U + step * U + u + 1)
                            nc.scalar.activation(O[:, u * D:(u + 1) * D], main[u % 4][:, 0:D], ACT.Copy,
                                                 scale=0.9 if mode == "smooth" else 1.0).then_inc(emptied.sem, 1)
                            if mode == "smooth":
                                t = n * U + u
                                last = nc.scalar.activation(own[:, u * D:(u + 1) * D], self.T[:, at_cols(t * D, D)],
                                                            ACT.Copy, scale=self.self_c[:, at_cols(t, 1)])
                                if u == h * H and follows is not None:
                                    act.wait_ge(scaled.sem, scaled.at + step * 2 + h + 1)
                                    act.sem_inc(self.turns_act, 1)
                                    fetch(follows, h)
                        if mode == "smooth":
                            last.then_inc(ready.sem, 1)
                    if is_last:
                        for h in range(2):
                            half_of(0, h, None)
                        with act.Fori(1, NI) as n:
                            for h in range(2):
                                half_of(n, h, None)
                    else:
                        with act.Fori(0, NI - 1) as n:
                            for h in range(2):
                                half_of(n, h, n + 1)
                        for h in range(2):
                            half_of(NI - 1, h, 0)
                if mode == "smooth":
                    for h in range(2):
                        fetch(0, h)
                rounds(act, one)

            @block.vector
            def _(dve):
                nc.vector.memset(carry[1][0:1, 0:D], 0.0).then_inc(linked.sem, 1)
                dve.wait_ge(linked.sem, linked.at + 1)

                def one(p, par, is_first, is_last):
                    def build(n, u):
                        t = n * U + u
                        dve.wait_ge(multiplied.sem, multiplied.at + p * NT + t + 1)
                        nc.vector.tensor_scalar(S[:, u * P:(u + 1) * P], self.rows[:, at_cols(t * P, P)],
                                                key[:, at_cols(t, 1)], weight[:, at_cols(t, 1)],
                                                ALU.is_equal, ALU.mult)

                    def carry_on(n, u):
                        step = p * NI + n
                        tile = step * U + u
                        slot = G[:, u * D:(u + 1) * D]
                        dve.wait_ge(filled[u], at + step * 16 + 16)
                        if mode == "mul":
                            nc.vector.tensor_mul(slot, slot, self.T[:, at_cols((n * U + u) * D, D)]
                                                 ).then_inc(gated.sem, 1)
                            dve.wait_ge(gated.sem, gated.at + tile + 1)
                        dve.wait_ge(carry_made.sem, carry_made.at + tile)
                        nc.vector.tensor_copy(slot[0:1, :], carry[(u + 1) % 2][0:1, 0:D]).then_inc(carried.sem, 1)

                    def renew(n, h):
                        step = p * NI + n
                        half = O[:, h * HD:(h + 1) * HD]
                        there = self.T[:, at_cols((n * U + h * H) * D, HD)]
                        if mode == "power":
                            dve.wait_ge(emptied.sem, emptied.at + 4 + step * U + (h + 1) * H)
                            if is_first:
                                dve.sem_inc(self.turns_dve, 1)
                                nc.vector.tensor_copy(there, half).then_inc(updated[h].sem, 1)
                            elif is_last:
                                nc.vector.scalar_tensor_tensor(out=half, in0=there, scalar=0.1, in1=half,
                                                               op0=ALU.mult, op1=ALU.add).then_inc(updated[h].sem, 1)
                            else:
                                nc.vector.tensor_add(there, there, half).then_inc(updated[h].sem, 1)
                        if mode == "smooth":
                            so_far = linked.at + 1 + 4 * step + 2 * h
                            dve.wait_ge(ready.sem, ready.at + step * 2 + h + 1)
                            nc.vector.tensor_add(half, half, own[:, h * HD:(h + 1) * HD]).then_inc(linked.sem, 1)
                            dve.wait_ge(linked.sem, so_far + 1)
                            if is_last:
                                nc.vector.tensor_add(half, half, x01[:, h * HD:(h + 1) * HD]).then_inc(linked.sem, 1)
                                dve.wait_ge(linked.sem, so_far + 2)
                                nc.vector.tensor_sub(half, half, xs[:, h * HD:(h + 1) * HD]
                                                     ).then_inc(updated[h].sem, 1)
                            else:
                                nc.vector.tensor_add(there, half, x01[:, h * HD:(h + 1) * HD]
                                                     ).then_inc(updated[h].sem, 1)
                                dve.sem_inc(linked.sem, 1)

                    def step_of(n, begins, ends):
                        for u in range(H):
                            carry_on(n, u)
                            build(n, H + u)
                        if not begins:
                            renew(n - 1, 1)
                        for u in range(H):
                            carry_on(n, H + u)
                            if not ends:
                                build(n + 1, u)
                        renew(n, 0)
                        if ends:
                            renew(n, 1)
                    for u in range(H):
                        build(0, u)
                    step_of(0, True, False)
                    with dve.Fori(1, NI - 1) as n:
                        step_of(n, False, False)
                    step_of(NI - 1, False, True)
                rounds(dve, one)

            if update:
                @block.sync
                def _(sp):
                    def one(p, par, is_first, is_last):
                        places = None if is_last else tables[table_at + par * TROWS:table_at + (par + 1) * TROWS, :].rearrange(
                            "(p t) d -> p (t d)", p=P)
                        with sp.Fori(0, NI) as n:
                            step = p * NI + n
                            for h in range(2):
                                if is_last:
                                    continue
                                cols = bass.ds((n * U + h * H) * D, HD)
                                if mode == "power":
                                    sp.wait_ge(emptied.sem, emptied.at + 4 + step * U + (h + 1) * H)
                                    sp.dma_start(places[:, cols], O[:, h * HD:(h + 1) * HD]
                                                 ).then_inc(stored[h].sem, 16)
                                else:
                                    sp.wait_ge(updated[h].sem, updated[h].at + step + 1)
                                    sp.dma_start(places[:, cols], self.T[:, cols]).then_inc(stored[h].sem, 16)
                    rounds(sp, one)
                    for h in range(2):
                        sp.wait_ge(stored[h].sem, stored[h].at + (K - 1) * 16 * NI)
        tiles = K * NT
        self.filled_at += K * NI * 16
        picked.at += K * 2 * NI
        placed.at += 2 * NI
        multiplied.at += tiles + U
        carry_made.at += tiles
        carried.at += tiles
        emptied.at += tiles + 4
        gated.at += tiles * (mode == "mul")
        linked.at += 1 + (4 * K * NI if mode == "smooth" else 0)
        ready.at += 2 * K * NI * (mode == "smooth")
        scaled.at += 2 * K * NI * (mode == "smooth")
        for h in range(2):
            updated[h].at += K * NI * update
            stored[h].at += (K - 1) * 16 * NI
            sent[h].at += 16 * H * NI
            landed[h].at += K * NI * 16 * (mode == "smooth")

    def dense(self, kind):
        nc, i = self.nc, self.i
        W = J * D
        B = 4
        R4 = 4
        x2 = self.tab2[0:N, :]
        first = {"d0": i["x"], "d1": self.x1, "d2": x2, "d3": self.z1, "d4": self.z2}[kind]
        agg = self.agg_s if kind == "d1" else self.agg_d
        norm_to = {"d0": self.x1, "d1": x2, "d2": self.x3, "d4": self.out}.get(kind)
        product_to = {"d2": self.z1, "d3": self.z2}.get(kind)
        normed = norm_to is not None
        conv = kind in ("d3", "d4")
        loads = 3 if kind == "d4" else 2
        names = ("read", "turned", "copied", "product", "summed", "centred", "squared", "spread", "rooted", "inverted", "divided",
                 "shifted", "scaled", "active", "kept", "inner")
        sig = {n: self.shared(f"dense_{n}") for n in names}
        read, turned, copied, product, summed, centred, squared, spread, rooted, inverted, divided, shifted, scaled, active, kept, inner = (
            sig[n] for n in names)
        landed = [self.shared(f"dense_landed{b}") for b in range(B)]
        stored = [self.shared(f"dense_stored{b}") for b in range(B)]
        zstored = [self.shared(f"dense_zstored{b}") for b in range(B)]
        wts = self.shared("dense_weights")
        const = self.shared("dense_const")
        rows = lambda t: t.rearrange("(p j) d -> p (j d)", p=NP_)
        LMAX = 8

        def run(eng, parts):
            def turn(it, j):
                for lag, fn in parts:
                    if isinstance(it, int) and not 0 <= it - lag < NG:
                        continue
                    fn(it - lag, (j - lag) % B)
            for it in range(LMAX):
                turn(it, it)
            loops = (NG - LMAX) // B
            with eng.Fori(0, loops) as k:
                for j in range(B):
                    turn(k * B + (LMAX + j), LMAX + j)
            for it in range(LMAX + loops * B, NG + LMAX):
                turn(it, it)

        with ExitStack() as s:
            def tmp(n, shape, dt=fp32):
                return s.enter_context(nc.sbuf_tensor(f"{kind}_{n}", shape, dt))

            X, A, Rr = tmp("X", [NP_, B * W]), tmp("A", [NP_, B * W]), tmp("R", [NP_, B * W])
            if normed:
                C, Q = tmp("C", [NP_, B * W]), tmp("Q", [NP_, B * W])
            mean, var, std, inv = (tmp(n, [NP_, B * J]) for n in ("mean", "var", "std", "inv"))
            eps = tmp("eps", [P, 1])
            if kind == "d0":
                xt = tmp("xt", [D + 2, 2 * J * NP_])
                at_ = tmp("at", [D, 2 * J * NP_])
                wa, wb = tmp("wa", [D + 2, D]), tmp("wb", [D, D])
            if product_to is not None:
                xt = tmp("xt", [D, 2 * J * NP_])
                wa = tmp("wa", [D, D])
                Z = tmp("Z", [NP_, B * W])
            if conv:
                dinv = tmp("dinv", [NP_, NJ])
                bias, slope = tmp("bias", [NP_, D]), tmp("slope", [NP_, D])
            if kind == "d4":
                X3 = tmp("X3", [NP_, B * W])
            n_w = {"d0": 4, "d1": 0, "d2": 1, "d3": 4, "d4": 3}[kind]

            def v2(x, b):
                return x[:, b * W:(b + 1) * W]

            def v3(x, b):
                return v2(x, b).rearrange("p (j d) -> p j d", d=D)

            def per_row(x, b):
                return x[:, b * J:(b + 1) * J].unsqueeze(2).to_broadcast([NP_, J, D])

            def per_feature(x):
                return x[:, :].unsqueeze(1).to_broadcast([NP_, J, D])

            def data(sg, g, b, m=1):
                return sg.at + (g - b) * (16 // B) * m + 16 * m

            def before(sg, g, b, m=1):
                return sg.at + (g - b) * (16 // B) * m

            if True:
                def load(g, b):
                    eng = nc.sync
                    hold(eng, read.sem, read.at + g + 1, self.turns_sp)
                    cols = bass.ds(g * W, W) if not isinstance(g, int) else slice(g * W, (g + 1) * W)
                    eng.dma_start(v2(X, b), rows(first)[:, cols]).then_inc(landed[b].sem, 16)
                    eng.dma_start(v2(A, b), rows(agg)[:, cols]).then_inc(landed[b].sem, 16)
                    if kind == "d4":
                        eng.dma_start(v2(X3, b), rows(self.x3)[:, cols]).then_inc(landed[b].sem, 16)

                def store(g, b):
                    eng = nc.sync
                    hold(eng, divided.sem, divided.at + g + 1 + B, self.turns_sp)
                    cols = bass.ds(g * W, W) if not isinstance(g, int) else slice(g * W, (g + 1) * W)
                    eng.dma_start(rows(norm_to)[:, cols], v2(C, b)).then_inc(stored[b].sem, 16)

                def store_z(g, b):
                    eng = nc.sync
                    hold(eng, kept.sem, kept.at + g * 2 + 2 + 4, self.turns_sp)
                    cols = bass.ds(g * W, W) if not isinstance(g, int) else slice(g * W, (g + 1) * W)
                    eng.dma_start(rows(product_to)[:, cols], v2(Z, b)).then_inc(zstored[b].sem, 16)

            block = s.enter_context(nc.Block())

            @block.sync
            def _(sp):
                n = 0
                with nc.allow_non_contiguous_dma(reason="weights are transposed once"):
                    def weight(to, of):
                        nonlocal n
                        sp.dma_start(to, of).then_inc(wts.sem, 16)
                        n += 1
                    if kind == "d0":
                        weight(wa[0:D, :], i["Ws"].rearrange("c k -> k c"))
                        weight(wa[D:D + 1, :], i["bs"].rearrange("(a c) -> a c", a=1))
                        weight(wa[D + 1:D + 2, :], i["bn"].rearrange("(a c) -> a c", a=1))
                        weight(wb[:, :], i["Wn"].rearrange("c k -> k c"))
                    if kind == "d2":
                        weight(wa[:, :], i["V1"])
                    if kind == "d3":
                        weight(wa[:, :], i["V2"])
                    if conv:
                        weight(dinv[:, :], self.dinv_n[0:N, :].rearrange("(p j) a -> p (j a)", p=NP_))
                        weight(bias[:, :], i["c1" if kind == "d3" else "c2"].partition_broadcast(NP_))
                        weight(slope[:, :], i["prelu_a"].partition_broadcast(NP_))
                assert n == n_w
                parts = [(0, load)]
                if normed:
                    parts.append((6, store))
                if product_to is not None:
                    parts.append((8 if kind == "d2" else 5, store_z))
                run(sp, parts)
                for b in range(B):
                    groups = len(range(b, NG, B))
                    if normed:
                        sp.wait_ge(stored[b].sem, stored[b].at + 16 * groups)
                    if product_to is not None:
                        sp.wait_ge(zstored[b].sem, zstored[b].at + 16 * groups)

            mm_from = {"d0": 2, "d2": 7, "d3": 4}.get(kind)

            @block.tensor
            def _(pe):
                if mm_from is None:
                    return
                pe.sem_inc(product.sem, 2)
                pe.wait_ge(wts.sem, wts.at + 16 * n_w)
                pe.wait_ge(const.sem, const.at + 2)

                def turn(g, b):
                    if kind == "d0":
                        pe.wait_ge(landed[b].sem, data(landed[b], g, b, 2))
                        sources = (X, A)
                    elif kind == "d2":
                        pe.wait_ge(divided.sem, divided.at + g + 1 + B)
                        sources = (C,)
                    else:
                        pe.wait_ge(active.sem, active.at + g + 1)
                        sources = (Rr,)
                    pe.wait_ge(copied.sem, copied.at + g * 2 * len(sources) + 2 * B)
                    k = 0
                    for src in sources:
                        for half in range(2):
                            for j in range(R4):
                                c0 = b * W + (half * R4 + j) * D
                                last = nc.tensor.transpose(self.bank[k][0:D, j * NP_:(j + 1) * NP_],
                                                           src[:, c0:c0 + D], self.ident[0:NP_, 0:NP_])
                            last.then_inc(turned.sem, 1)
                            k += 1

                def mult(g, b):
                    n_src = 2 if kind == "d0" else 1
                    pe.wait_ge(copied.sem, copied.at + g * 2 * n_src + 2 * n_src + 2 * B)
                    if kind == "d0":
                        pe.wait_ge(read.sem, read.at + g + B - 1)
                    else:
                        pe.wait_ge(kept.sem, kept.at + g * 2 + 2)
                    b2 = b % 2
                    for half in range(2):
                        for j in range(R4):
                            r = (b2 * J + half * R4 + j) * NP_
                            o = self.bank[4 + b2 * 2 + half][0:NP_, j * D:(j + 1) * D]
                            if kind == "d0":
                                nc.tensor.matmul(o, xt[:, r:r + NP_], wa[:, :], start=True, stop=False)
                                last = nc.tensor.matmul(o, at_[:, r:r + NP_], wb[:, :], start=False, stop=True)
                            else:
                                last = nc.tensor.matmul(o, xt[:, r:r + NP_], wa[:, :], start=True, stop=True)
                    last.then_inc(product.sem, 1)
                run(pe, [(mm_from + 1, mult), (mm_from, turn)])

            @block.scalar
            def _(act):
                def copy(g, b):
                    b2 = b % 2
                    act.wait_ge(product.sem, product.at + g + 1)
                    k = 0
                    n_src = 2 if kind == "d0" else 1
                    for to in ((xt, at_) if kind == "d0" else (xt,)):
                        for half in range(2):
                            act.wait_ge(turned.sem, turned.at + g * 2 * n_src + k + 1)
                            c0 = (b2 * J + half * R4) * NP_
                            nc.scalar.activation(to[0:D, c0:c0 + R4 * NP_], self.bank[k][0:D, 0:R4 * NP_], ACT.Copy
                                                 ).then_inc(copied.sem, 1)
                            k += 1

                def square(g, b):
                    act.wait_ge(centred.sem, centred.at + g + 1 + B)
                    act.wait_ge(spread.sem, spread.at + g + 1)
                    nc.scalar.activation(v2(Q, b), v2(C, b), ACT.Square).then_inc(squared.sem, 1)

                def root(g, b):
                    act.wait_ge(spread.sem, spread.at + g + 1 + B)
                    act.wait_ge(inverted.sem, inverted.at + g + 1)
                    nc.scalar.activation(std[:, b * J:(b + 1) * J], var[:, b * J:(b + 1) * J], ACT.Sqrt,
                                         bias=eps[0:NP_, :], scale=1.0 / D).then_inc(rooted.sem, 1)

                def scale_agg(g, b):
                    act.wait_ge(landed[b].sem, data(landed[b], g, b, 2))
                    nc.scalar.activation(v2(A, b), v2(A, b), ACT.Copy, scale=1.0 / THETA).then_inc(scaled.sem, 1)

                def keep(g, b):
                    b2 = b % 2
                    act.wait_ge(product.sem, product.at + g + 1 + 2)
                    act.wait_ge(zstored[b].sem, before(zstored[b], g, b))
                    for half in range(2):
                        c0 = b * W + half * R4 * D
                        nc.scalar.activation(Z[:, c0:c0 + R4 * D], self.bank[4 + b2 * 2 + half][0:NP_, 0:R4 * D],
                                             ACT.Copy).then_inc(kept.sem, 1)
                act.wait_ge(const.sem, const.at + 2)
                act.sem_inc(copied.sem, 2 * B)
                act.sem_inc(kept.sem, 4)
                act.sem_inc(rooted.sem, B)
                parts = [(5, root), (4, square)] if normed else []
                if product_to is not None:
                    parts.append((mm_from + 1, keep))
                if mm_from is not None:
                    parts.append((mm_from, copy))
                if kind == "d1":
                    parts.append((2, scale_agg))
                run(act, parts)

            @block.vector
            def _(dve):
                nc.vector.memset(eps[:, :], 1e-5).then_inc(const.sem, 1)
                if kind == "d0":
                    nc.vector.memset(xt[D:D + 2, :], 1.0).then_inc(const.sem, 1)
                else:
                    dve.sem_inc(const.sem, 1)
                dve.sem_inc(read.sem, B)
                dve.sem_inc(spread.sem, B)
                dve.sem_inc(inverted.sem, B)
                if conv:
                    dve.wait_ge(wts.sem, wts.at + 16 * n_w)
                steps = {"d0": 3, "d1": 2, "d2": 2, "d3": 3, "d4": 6}[kind]

                def residual(g, b):
                    done = [0]

                    def link(ins):
                        done[0] += 1
                        ins.then_inc(inner.sem, 1)
                        dve.wait_ge(inner.sem, inner.at + g * steps + done[0])
                    if normed:
                        dve.wait_ge(centred.sem, centred.at + g + 1)
                    else:
                        dve.wait_ge(copied.sem, copied.at + g * 2 + 2)
                    dve.wait_ge(landed[b].sem, data(landed[b], g, b, loads))
                    v = nc.vector
                    if kind == "d0":
                        dve.wait_ge(product.sem, product.at + g + 1 + 2)
                        for half in range(2):
                            c0 = b * W + half * R4 * D
                            link(v.scalar_tensor_tensor(out=Rr[:, c0:c0 + R4 * D],
                                                        in0=self.bank[4 + (b % 2) * 2 + half][0:NP_, 0:R4 * D],
                                                        scalar=0.0, in1=X[:, c0:c0 + R4 * D], op0=ALU.max, op1=ALU.add))
                    elif kind == "d1":
                        dve.wait_ge(scaled.sem, scaled.at + g + 1)
                        link(v.scalar_tensor_tensor(out=v2(Rr, b), in0=v2(X, b), scalar=1.0 + 0.1 / THETA,
                                                    in1=v2(A, b), op0=ALU.mult, op1=ALU.add))
                    elif kind == "d2":
                        link(v.scalar_tensor_tensor(out=v2(Rr, b), in0=v2(X, b), scalar=2.0, in1=v2(A, b),
                                                    op0=ALU.mult, op1=ALU.add))
                    else:
                        cols = bass.ds(g * J, J) if not isinstance(g, int) else slice(g * J, (g + 1) * J)
                        link(v.tensor_tensor(out=v3(Rr, b), in0=v3(X, b),
                                             in1=dinv[:, cols].unsqueeze(2).to_broadcast([NP_, J, D]), op=ALU.mult))
                        dve.wait_ge(shifted.sem, shifted.at + g + 1)
                        link(v.tensor_add(v2(Rr, b), v2(Rr, b), v2(A, b)))
                        link(v.scalar_tensor_tensor(out=v3(A, b), in0=v3(Rr, b), scalar=0.0, in1=per_feature(slope),
                                                    op0=ALU.min, op1=ALU.mult))
                        last = v.scalar_tensor_tensor(out=v2(Rr, b), in0=v2(Rr, b), scalar=0.0, in1=v2(A, b),
                                                      op0=ALU.max, op1=ALU.add)
                        if kind == "d3":
                            last.then_inc(active.sem, 1)
                            dve.wait_ge(active.sem, active.at + g + 1)
                            dve.sem_inc(read.sem, 1)
                            return
                        link(last)
                        link(v.tensor_add(v2(Rr, b), v2(Rr, b), v2(X3, b)))
                    dve.sem_inc(read.sem, 1)
                    link(v.tensor_reduce(out=mean[:, b * J:(b + 1) * J], in_=v3(Rr, b), axis=AXX, op=ALU.add))
                    v.tensor_single_scalar(mean[:, b * J:(b + 1) * J], mean[:, b * J:(b + 1) * J], -1.0 / D,
                                           op=ALU.mult).then_inc(summed.sem, 1)

                def variance(g, b):
                    dve.wait_ge(squared.sem, squared.at + g + 1)
                    dve.wait_ge(rooted.sem, rooted.at + g + 1)
                    nc.vector.tensor_reduce(out=var[:, b * J:(b + 1) * J], in_=v3(Q, b), axis=AXX, op=ALU.add
                                            ).then_inc(spread.sem, 1)
                def invert(g, b):
                    dve.wait_ge(rooted.sem, rooted.at + g + 1 + B)
                    dve.wait_ge(divided.sem, divided.at + g + 1)
                    nc.vector.reciprocal(inv[:, b * J:(b + 1) * J], std[:, b * J:(b + 1) * J]).then_inc(inverted.sem, 1)
                run(dve, ([(6, invert), (5, variance)] if normed else []) + [(3, residual)])

            @block.gpsimd
            def _(pool):
                if normed:
                    pool.sem_inc(centred.sem, B)
                    pool.sem_inc(divided.sem, B)
                if conv:
                    pool.wait_ge(wts.sem, wts.at + 16 * n_w)

                def shift(g, b):
                    pool.wait_ge(landed[b].sem, data(landed[b], g, b, loads))
                    nc.gpsimd.tensor_tensor(out=v3(A, b), in0=v3(A, b), in1=per_feature(bias), op=ALU.add
                                            ).then_inc(shifted.sem, 1)

                def centre(g, b):
                    hold(pool, stored[b].sem, before(stored[b], g, b), self.turns)
                    if kind == "d2":
                        hold(pool, copied.sem, copied.at + g * 2 + 2, self.turns)
                    pool.wait_ge(summed.sem, summed.at + g + 1)
                    nc.gpsimd.tensor_tensor(out=v3(C, b), in0=v3(Rr, b), in1=per_row(mean, b), op=ALU.add
                                            ).then_inc(centred.sem, 1)

                def divide(g, b):
                    pool.wait_ge(inverted.sem, inverted.at + g + 1 + B)
                    nc.gpsimd.tensor_tensor(out=v3(C, b), in0=v3(C, b), in1=per_row(inv, b), op=ALU.mult
                                            ).then_inc(divided.sem, 1)
                parts = [(6, divide), (4, centre)] if normed else []
                if conv:
                    parts.append((2, shift))
                run(pool, parts)
        n_src = 2 if kind == "d0" else 1
        read.at += NG + B
        const.at += 2
        wts.at += 16 * n_w
        inner.at += NG * {"d0": 3, "d1": 2, "d2": 2, "d3": 3, "d4": 6}[kind]
        spread.at += B + NG * normed
        rooted.at += B + NG * normed
        inverted.at += B + NG * normed
        copied.at += 2 * B + (2 * n_src * NG if mm_from is not None else 0)
        kept.at += 4 + 2 * NG * (product_to is not None)
        for sg in (summed, squared):
            sg.at += NG * normed
        for sg in (centred, divided):
            sg.at += (NG + B) * normed
        if mm_from is not None:
            turned.at += 2 * n_src * NG
            product.at += NG + 2
        shifted.at += NG * conv
        active.at += NG * (kind == "d3")
        scaled.at += NG * (kind == "d1")
        for b in range(B):
            groups = 16 * len(range(b, NG, B))
            landed[b].at += groups * loads
            stored[b].at += groups * normed
            zstored[b].at += groups * (product_to is not None)


def build_program(nc, x, src, dst, edge_attr_17, W1, b1, W2, b2, Ws, bs, Wn, bn, V1, c1, V2, c2, prelu_a, out):
    ins = dict(x=x, src=src, dst=dst, ea=edge_attr_17, W1=W1, b1=b1, W2=W2, b2=b2, Ws=Ws, bs=bs, Wn=Wn, bn=bn,
               V1=V1, c1=c1, V2=V2, c2=c2, prelu_a=prelu_a)
    with ExitStack() as ctx:
        Program(nc, ctx, ins, out).build()


_INS = ['x', 'src', 'dst', 'edge_attr_17', 'L0_gnn_W1', 'L0_gnn_b1', 'L0_gnn_W2', 'L0_gnn_b2', 'L0_gnn_Ws', 'L0_gnn_bs',
        'L0_gnn_Wn', 'L0_gnn_bn', 'L3_gnn_W1', 'L3_gnn_b1', 'L3_gnn_W2', 'L3_gnn_b2', 'L3_gnn_prelu_a']
_OUTS = [((N, D), 'float32')]


def kernel(**inputs):
    import numpy as _np
    import concourse.bacc as _bacc
    from concourse import mybir as _mybir
    from concourse.bass_utils import run_bass_kernel_spmd as _run

    nc = _bacc.Bacc("TRN2", target_bir_lowering=False, num_devices=1)
    arrays, args = {}, []
    for name in _INS:
        a = _np.ascontiguousarray(inputs[name])
        arrays[f"in_{name}_dram"] = a
        args.append(nc.dram_tensor(f"in_{name}_dram", a.shape, _mybir.dt.from_np(a.dtype), kind="ExternalInput").ap())
    for i, (shape, dtype) in enumerate(_OUTS):
        dt = _mybir.dt.from_np(_np.dtype(dtype))
        args.append(nc.dram_tensor(f"out_{i}_dram", shape, dt, kind="ExternalOutput").ap())
    build_program(nc, *args)
    r = _run(nc, [arrays], core_ids=[0])
    return r.results[0]["out_0_dram"]
```

```python
from contextlib import ExitStack

import concourse.bass as bass
import numpy as np
from concourse import mybir

fp32 = mybir.dt.float32
bf16 = mybir.dt.bfloat16
i32 = mybir.dt.int32
ALU = mybir.AluOpType
ACT = mybir.ActivationFunctionType
AXX = mybir.AxisListType.X

N, E, D, ED = 50000, 25000, 96, 17
P = 128
EP = P - 1
U = 8
H = U // 2
NI = -(-(-(-E // EP)) // U)
NT = NI * U
UP = 10
CH = NT // 2
FULL = E // EP
REST = E - FULL * EP
PAD = 65000.0
BIG = 1 << 20
TROWS = P * NT
LO = 256
HP = 98
NODES = HP * 2 * LO
MAGIC = 12582912.0
MF = 8
F_IN, F_OUT, F_DEND, F_SSTART, F_L2, F_L1 = range(6)
R_KEY, R_COL, R_W, R_L1, R_TGT = range(5)
NP_ = 125
NJ = N // NP_
J = 8
NG = NJ // J
ZROWS = LO
ZJ = 25
K1, K2 = 10, 16
BETA = 0.9
THETA = BETA ** K1 + 0.1 * sum(BETA ** i for i in range(K1))


def hold(eng, sem, value, turns):
    eng.wait_ge(sem, value)
    eng.sem_inc(turns, 1)


class Signal:

    def __init__(self, sem, first):
        self.sem, self.at = sem, first


class Chain:

    def __init__(self, eng, sem):
        self.eng, self.sem, self.n = eng, sem, 0

    def __call__(self, instruction):
        self.n += 1
        instruction.then_inc(self.sem, 1)
        self.eng.wait_ge(self.sem, self.n)


class Program:

    def __init__(self, nc, ctx, ins, out):
        self.nc, self.ctx, self.i, self.out = nc, ctx, ins, out
        self.turns = self.sem("turns_pool")
        self.turns_act = self.sem("turns_act")
        self.turns_dve = self.sem("turns_dve")
        self.turns_sp = self.sem("turns_sp")
        self.turns_pe = self.sem("turns_pe")
        self.counters, self.fresh = {}, []
        self.filled = [self.shared(f"slot_filled{u}", pool_dma=True) for u in range(UP)]

    def sem(self, name):
        return self.ctx.enter_context(self.nc.semaphore(name))

    def shared(self, name, dma=False, pool_dma=False):
        if name not in self.counters:
            self.counters[name] = Signal(self.sem(name), 0 if pool_dma else 16 if dma else 1)
            if not pool_dma:
                self.fresh.append(self.counters[name])
        return self.counters[name]

    def start(self, eng):
        for s in self.fresh:
            eng.sem_inc(s.sem, s.at)
        self.fresh = []

    def dram(self, name, shape, dt=fp32):
        return self.nc.dram_tensor(name, shape, dt).ap()

    def build(self):
        nc, ctx = self.nc, self.ctx

        def sb(name, shape, dt=fp32):
            return ctx.enter_context(nc.sbuf_tensor(name, shape, dt))

        self.bank = [ctx.enter_context(nc.psum_tensor(f"bank{b}", [P, 512], fp32)) for b in range(8)]
        self.ident = sb("ident", [P, P])
        self.src_i = sb("src_i", [P, NT], i32)
        self.dst_i = sb("dst_i", [P, NT], i32)
        self.key_d = sb("key_d", [P, NT])
        self.ones_d = sb("ones_d", [P, NT])
        self.norm = sb("norm", [P, NT])
        self.self_c = sb("self_c", [P, NT])
        self.tgt_d = sb("tgt_d", [P, NT], i32)
        self.l2 = [sb(f"l2_{k}", [P, NT], i32) for k in range(2)]
        self.key_s = sb("key_s", [P, NT])
        self.w_s = sb("w_s", [P, NT])
        self.col_i = sb("col_i", [P, NT], i32)
        self.tgt_s = sb("tgt_s", [P, NT], i32)
        self.l1 = [sb(f"l1_{k}", [P, NT], i32) for k in range(2)]
        self.G = sb("G", [P, UP * D])
        self.O = sb("O", [P, UP * D])
        self.cur = sb("cur", [P, 2 * UP], i32)

        self.brow_d = self.dram("brow_d", [NT, P])
        self.brow_s = self.dram("brow_s", [NT, P])
        self.srow = self.dram("srow", [NT, P])
        self.hrow = self.dram("hrow", [NT, P])
        self.meta = self.dram("meta", [NODES, MF])
        self.rec = self.dram("rec", [TROWS, MF])
        self.agg_d = self.dram("agg_d", [N, D])
        self.agg_s = self.dram("agg_s", [N, D])
        self.x1 = self.dram("x1", [N, D])
        self.tab1 = self.dram("tab1", [2 * TROWS + ZROWS, D])
        self.tab2 = self.dram("tab2", [2 * TROWS + N, D])
        self.xp = self.dram("xp", [P, NT * D])
        self.x3 = self.dram("x3", [N, D])
        self.z1 = self.dram("z1", [N, D])
        self.z2 = self.dram("z2", [N, D])
        self.dinv_n = self.dram("dinv_n", [NODES, 1])

        with ExitStack() as s:
            self.T = s.enter_context(nc.sbuf_tensor("T0", [P, NT * D], fp32))
            with ExitStack() as s2:
                def tmp(name, shape, dt=fp32):
                    return s2.enter_context(nc.sbuf_tensor(name, shape, dt))

                self.src_f = tmp("src_f", [P, NT])
                self.load_edges()
                self.cnt = tmp("cnt", [P, NT])
                self.ms = tmp("ms", [P, NT * MF])
                self.md = tmp("md", [P, NT * MF])
                self.count_edges()
                self.gather_rows("ms", self.meta, self.src_i, MF, self.ms, clear=(
                    (self.agg_d, NP_), (self.agg_s, NP_), (self.tab1[2 * TROWS:2 * TROWS + ZROWS, :], P)))
                self.gather_rows("md", self.meta, self.dst_i, MF, self.md, clear=(
                    (self.tab1[TROWS:2 * TROWS, :], P), (self.tab2[N:N + 2 * TROWS, :], P)))
                self.edge_records()
            self.rows = s.enter_context(nc.sbuf_tensor("rows_l0", [P, NT * P], fp32))
            self.load_records(self.brow_d)
            self.passes("l0", "mul")
        with ExitStack() as s:
            self.rows = s.enter_context(nc.sbuf_tensor("rows", [P, NT * P], fp32))
            self.dense("d0", self.brow_s)
            with ExitStack() as s2:
                self.T = s2.enter_context(nc.sbuf_tensor("T1", [P, NT * D], fp32))
                self.passes("l1", "power")
            self.dense("d1", self.brow_d)
            with ExitStack() as s2:
                self.T = s2.enter_context(nc.sbuf_tensor("T2", [P, NT * D], fp32))
                self.gather_rows("t2", self.tab2, self.dst_i, D, self.T, self.xp)
                self.passes("l2", "smooth")
            self.dense("d2")
            self.passes("l3a", "plain", self.z1)
            self.dense("d3")
            self.passes("l3b", "plain", self.z2)
        self.dense("d4")

    def load_edges(self):
        nc, i = self.nc, self.i
        with ExitStack() as s:
            def tmp(name, shape, dt=fp32):
                return s.enter_context(nc.sbuf_tensor(name, shape, dt))

            rows = [tmp(f"rows{k}", [CH, 2, P], i32) for k in range(2)]
            rowf = [tmp(f"rowf{k}", [CH, 2, P]) for k in range(2)]
            rowb = tmp("rowb", [CH, 2, P])
            high_i = tmp("high_i", [CH, 2, P], i32)
            high = tmp("high", [CH, 2, P])
            blank, landed, made, turned, stored, chain = (self.sem(f"load_{n}") for n in
                                                           ("blank", "landed", "made", "turned", "stored", "chain"))
            identity = self.sem("load_identity")
            flat = [i["src"], i["dst"]]
            block = s.enter_context(nc.Block())

            @block.gpsimd
            def _(pool):
                nc.gpsimd.memset(self.ident[:, :], 0.0).then_inc(identity, 1)
                pool.wait_ge(identity, 1)
                nc.gpsimd.affine_select(out=self.ident[:, :], in_=self.ident[:, :], compare_op=ALU.not_equal, fill=1.0,
                                        base=0, pattern=[[-1, P]], channel_multiplier=1).then_inc(identity, 1)

            @block.sync
            def _(sp):
                sp.wait_ge(blank, 2)
                n = 0

                def load(to, of):
                    nonlocal n
                    sp.dma_start(to, of).then_inc(landed, 16)
                    n += 16

                with nc.allow_non_contiguous_dma(reason="one number of each tile"):
                    for k in range(2):
                        load(rows[k][0:CH, 0, 1:P], flat[k][0:CH * EP].rearrange("(p q) -> p q", q=EP))
                        load(rows[k][0:FULL - CH, 1, 1:P],
                             flat[k][CH * EP:FULL * EP].rearrange("(p q) -> p q", q=EP))
                        load(rows[k][FULL - CH:FULL - CH + 1, 1, 1:REST + 1],
                             flat[k][FULL * EP:E].rearrange("(p q) -> p q", p=1))
                    load(rows[1][1:CH, 0, 0:1],
                         flat[1][EP - 1:EP - 1 + (CH - 1) * EP].rearrange("(p q) -> p q", q=EP)[:, 0:1])
                    last = CH * EP - 1
                    load(rows[1][0:FULL - CH, 1, 0:1],
                         flat[1][last:last + (FULL - CH) * EP].rearrange("(p q) -> p q", q=EP)[:, 0:1])
                    load(rows[1][FULL - CH:FULL - CH + 1, 1, 0:1],
                         flat[1][FULL * EP - 1:FULL * EP].rearrange("(p q) -> p q", p=1))
                self.landed_edges = n
                sp.wait_ge(made, 1)
                for k, (to, of) in enumerate(((self.brow_d, rowb), (self.srow, rowf[0]), (self.hrow, high))):
                    sp.dma_start(to.rearrange("(c p) q -> p c q", c=2), of[:, :, :]).then_inc(stored, 16)
                sp.wait_ge(stored, 48)

            @block.vector
            def _(dve):
                link = Chain(dve, chain)
                for k in range(2):
                    nc.vector.memset(rows[k][:, :, :], int(PAD)).then_inc(blank, 1)
                dve.wait_ge(landed, 16 * 9)
                for k in range(2):
                    link(nc.vector.tensor_copy(rowf[k][:, :, :], rows[k][:, :, :]))
                link(nc.vector.tensor_single_scalar(high_i[:, :, :], rows[0][:, :, :], 8, op=ALU.logical_shift_right))
                link(nc.vector.tensor_copy(rowb[:, :, :], rowf[1][:, :, :]))
                link(nc.vector.tensor_copy(rowb[:, :, 0:1], rowf[1][:, :, P - 1:P]))
                nc.vector.tensor_copy(high[:, :, :], high_i[:, :, :]).then_inc(made, 1)
                dve.wait_ge(turned, 4)
                for k, to in enumerate((self.src_f, self.key_d)):
                    for c in range(2):
                        link(nc.vector.tensor_copy(to[:, c * CH:(c + 1) * CH], self.bank[2 * k + c][:, 0:CH]))
                for to, of in ((self.src_i, self.src_f), (self.dst_i, self.key_d)):
                    link(nc.vector.tensor_single_scalar(to[:, :], of[:, :], float(N - 1), op=ALU.min))

            @block.tensor
            def _(pe):
                pe.wait_ge(identity, 2)
                pe.wait_ge(made, 1)
                for k in range(2):
                    for c in range(2):
                        nc.tensor.transpose(self.bank[2 * k + c][:, 0:CH], rowf[k][:, c, :],
                                            self.ident[0:CH, 0:CH]).then_inc(turned, 1)

    def count_edges(self):
        nc = self.nc
        with ExitStack() as s:
            def tmp(name, shape, dt=fp32):
                return s.enter_context(nc.sbuf_tensor(name, shape, dt))

            dig_i = tmp("dig_i", [P, NT], i32)
            dig_t = tmp("dig_t", [P, NT], i32)
            hi, lo = [tmp(f"hi{k}", [P, NT]) for k in range(2)], [tmp(f"lo{k}", [P, NT]) for k in range(2)]
            iota_hi = tmp("iota_hi", [P, 2 * HP], bf16)
            iota_lo = tmp("iota_lo", [P, LO], bf16)
            iota_p = tmp("iota_p", [HP, 2])
            earlier = tmp("earlier", [P, P])
            zeros = tmp("zeros", [P, 2 * LO], bf16)
            hb = tmp("hb", [HP, 2, U * P])
            sbr = tmp("sbr", [P, 2, U * P])
            oht = tmp("oht", [HP, 2, 2, U * P], bf16)
            R4 = 4
            oh = [[tmp(f"oh{k}{u}", [P, 2 * HP], bf16) for u in range(R4)] for k in range(2)]
            ol = [[tmp(f"ol{k}{u}", [P, LO], bf16) for u in range(R4)] for k in range(2)]
            junk_n, junk_f = tmp("junk_n", [P, P]), tmp("junk_f", [P, LO])
            snap = [tmp(f"snap{u}", [HP, 2 * LO]) for u in range(2)]
            coarse = [tmp(f"coarse{u}", [HP, 2 * LO], bf16) for u in range(2)]
            fine = [tmp(f"fine{u}", [HP, 2 * LO], bf16) for u in range(2)]
            near, far = tmp("near", [P, NT]), tmp("far", [P, NT])
            hist = [self.bank[0][0:HP, :], self.bank[1][0:HP, :]]
            look = [self.bank[2][:, 0:LO], self.bank[3][:, 0:LO]]
            const, zeroed, chain = (self.sem(f"count_{n}") for n in ("const", "zeroed", "chain"))
            rows_in = [self.shared(f"count_rows{b}", True) for b in range(2)]
            onehot, ohts, product, snapped, rounded, split, looked, nears, fars = (
                self.shared(f"count_{n}") for n in ("onehot", "ohts", "product", "snapped", "rounded", "split",
                                                    "looked", "nears", "fars"))
            block = s.enter_context(nc.Block())

            def steps(eng, body):
                body(0, 0)
                with eng.Fori(0, (NI - 3) // 2) as k:
                    body(k * 2 + 1, 1)
                    body(k * 2 + 2, 0)
                body(NI - 2, 1)
                body(NI - 1, 0)

            @block.gpsimd
            def _(pool):
                self.start(pool)
                nc.gpsimd.iota(iota_hi[:, :], pattern=[[1, 2], [2, HP]], base=0, channel_multiplier=0,
                               allow_small_or_imprecise_dtypes=True).then_inc(const, 1)
                nc.gpsimd.iota(iota_lo[:, :], pattern=[[1, LO]], base=0, channel_multiplier=0,
                               allow_small_or_imprecise_dtypes=True).then_inc(const, 1)
                nc.gpsimd.iota(iota_p[:, :], pattern=[[1, 2]], base=0, channel_multiplier=2,
                               allow_small_or_imprecise_dtypes=True).then_inc(const, 1)
                nc.gpsimd.memset(earlier[:, :], 1.0).then_inc(const, 1)
                pool.wait_ge(const, 4)
                nc.gpsimd.affine_select(out=earlier[:, :], in_=earlier[:, :], compare_op=ALU.is_gt, fill=0.0,
                                        base=0, pattern=[[-1, P]], channel_multiplier=1).then_inc(const, 1)
                nc.gpsimd.memset(zeros[:, :], 0.0).then_inc(const, 1)

                def body(n, b):
                    for u in range(U):
                        hold(pool, rounded.sem, rounded.at + n * U + (u + 1), self.turns)
                        if not (isinstance(n, int) and n * U + u < 2):
                            hold(pool, looked.sem, looked.at + n * U + (u - 1), self.turns)
                        nc.gpsimd.tensor_sub(fine[u % 2][:, :], snap[u % 2][:, :], coarse[u % 2][:, :]
                                             ).then_inc(split.sem, 1)
                steps(pool, body)

            @block.sync
            def _(sp):
                def load(n, b):
                    rows = slice(n * U, (n + 1) * U) if isinstance(n, int) else bass.ds(n * U, U)
                    sp.dma_start(hb[:, b, :], self.hrow[rows, :].rearrange("t q -> (t q)").partition_broadcast(HP)
                                 ).then_inc(rows_in[b].sem, 16)
                    sp.dma_start(sbr[:, b, :], self.srow[rows, :].rearrange("t q -> (t q)").partition_broadcast(P)
                                 ).then_inc(rows_in[b].sem, 16)

                def body(n, b):
                    if not (isinstance(n, int) and n == 0):
                        sp.wait_ge(nears.sem, nears.at + n * U)
                        sp.sem_inc(self.turns_sp, 1)
                    if not (isinstance(n, int) and n == NI - 1):
                        load(n + 1, 1 - b)
                load(0, 0)
                steps(sp, body)

            @block.vector
            def _(dve):
                link = Chain(dve, chain)
                for k, key in enumerate((self.src_f, self.key_d)):
                    link(nc.vector.tensor_copy(dig_i[:, :], key[:, :]))
                    link(nc.vector.tensor_single_scalar(dig_t[:, :], dig_i[:, :], 8, op=ALU.logical_shift_right))
                    link(nc.vector.tensor_copy(hi[k][:, :], dig_t[:, :]))
                    link(nc.vector.tensor_single_scalar(dig_t[:, :], dig_i[:, :], LO - 1, op=ALU.bitwise_and))
                    link(nc.vector.tensor_copy(lo[k][:, :], dig_t[:, :]))
                link(nc.vector.memset(hi[1][0:1, :], -1.0))
                dve.wait_ge(const, 6)

                def col(t):
                    return slice(t, t + 1) if isinstance(t, int) else bass.ds(t, 1)

                def digits(t, u):
                    if not (isinstance(t, int) and t < R4):
                        dve.wait_ge(product.sem, product.at + t - (R4 - 1))
                        dve.wait_ge(fars.sem, fars.at + t - (R4 - 1))
                    for k in range(2):
                        nc.vector.tensor_scalar(oh[k][u % R4][:, :], iota_hi[:, :], hi[k][:, col(t)], None,
                                                ALU.is_equal).then_inc(onehot.sem, 1)
                        nc.vector.tensor_scalar(ol[k][u % R4][:, :], iota_lo[:, :], lo[k][:, col(t)], None,
                                                ALU.is_equal).then_inc(onehot.sem, 1)

                def pairs(t, u, b):
                    dve.wait_ge(nears.sem, nears.at + t)
                    nc.vector.scalar_tensor_tensor(
                        out=junk_n[:, :], in0=sbr[:, b, u * P:(u + 1) * P], scalar=self.src_f[:, col(t)],
                        in1=earlier[:, :], op0=ALU.is_equal, op1=ALU.mult, accum_out=near[:, col(t)]
                    ).then_inc(nears.sem, 1)

                def tiles_before(t, u):
                    dve.wait_ge(looked.sem, looked.at + t + 1)
                    dve.wait_ge(fars.sem, fars.at + t)
                    dve.wait_ge(onehot.sem, onehot.at + t * 4 + 4)
                    nc.vector.scalar_tensor_tensor(
                        out=junk_f[:, :], in0=look[u % 2], scalar=1.0, in1=ol[0][u % R4][:, :], op0=ALU.mult,
                        op1=ALU.mult, accum_out=far[:, col(t)]).then_inc(fars.sem, 1)

                def high_digits(n, b):
                    dve.wait_ge(rows_in[b].sem, rows_in[b].at + (n - b) * 16 + 32)
                    for c in range(2):
                        nc.vector.tensor_scalar(oht[:, b, c, :], hb[:, b, :], iota_p[:, c:c + 1], None,
                                                ALU.is_equal).then_inc(ohts.sem, 1)

                def body(n, b):
                    begins, ends = (isinstance(n, int) and n == k for k in (0, NI - 1))
                    for u in range(U):
                        t = n * U + u
                        pairs(t, u, b)
                        if not (ends and u == U - 1):
                            digits(t + 1, u + 1)
                        if not (begins and u < 2):
                            tiles_before(t - 2, u - 2)
                        if u == 5 and not ends:
                            high_digits(n + 1, 1 - b)
                    if ends:
                        tiles_before(NT - 2, U - 2)
                        tiles_before(NT - 1, U - 1)
                digits(0, 0)
                high_digits(0, 0)
                steps(dve, body)
                dve.wait_ge(fars.sem, fars.at + NT)
                dve.wait_ge(nears.sem, nears.at + NT)
                nc.vector.tensor_add(self.cnt[:, :], near[:, :], far[:, :]).then_inc(chain, 1)

            @block.tensor
            def _(pe):
                pe.wait_ge(const, 6)
                for k in range(2):
                    nc.tensor.matmul(hist[k], zeros[:, 0:HP], zeros[:, :], start=True, stop=True).then_inc(zeroed, 1)

                def count(t, u):
                    pe.wait_ge(snapped.sem, snapped.at + t + 1)
                    pe.wait_ge(onehot.sem, onehot.at + t * 4 + 4)
                    for k in range(2):
                        for c in range(2):
                            last = nc.tensor.matmul(hist[k][:, c * LO:(c + 1) * LO],
                                                    oh[k][u % R4][:, c * HP:(c + 1) * HP], ol[k][u % R4][:, :],
                                                    start=False, stop=True, skip_group_check=True)
                    last.then_inc(product.sem, 1)

                def lookup(t, u, b):
                    pe.wait_ge(split.sem, split.at + t + 1)
                    if not (isinstance(t, int) and t < 2):
                        pe.wait_ge(fars.sem, fars.at + t - 1)
                    k = 0
                    for c in range(2):
                        for part in (coarse, fine):
                            last = nc.tensor.matmul(look[u % 2], oht[:, b, c, u * P:(u + 1) * P],
                                                    part[u % 2][:, c * LO:(c + 1) * LO], start=k == 0, stop=k == 3)
                            k += 1
                    last.then_inc(looked.sem, 1)

                def body(n, b):
                    for u in range(U):
                        t = n * U + u
                        count(t, u)
                        if u > 0:
                            lookup(t - 1, u - 1, b)
                        elif not (isinstance(n, int) and n == 0):
                            lookup(t - 1, U - 1, 1 - b)
                        if u == 0:
                            pe.wait_ge(ohts.sem, ohts.at + n * 2 + 2)
                            pe.sem_inc(self.turns_pe, 1)
                    if isinstance(n, int) and n == NI - 1:
                        lookup(NT - 1, U - 1, b)
                steps(pe, body)

            @block.scalar
            def _(act):
                act.wait_ge(zeroed, 2)

                def body(n, b):
                    for u in range(U):
                        act.wait_ge(product.sem, product.at + n * U + u)
                        if not (isinstance(n, int) and n * U + u < 2):
                            act.wait_ge(split.sem, split.at + n * U + (u - 1))
                        nc.scalar.activation(snap[u % 2][:, :], hist[0], ACT.Copy).then_inc(snapped.sem, 1)
                        act.wait_ge(snapped.sem, snapped.at + n * U + (u + 1))
                        if not (isinstance(n, int) and n * U + u < 2):
                            act.wait_ge(looked.sem, looked.at + n * U + (u - 1))
                        nc.scalar.activation(coarse[u % 2][:, :], snap[u % 2][:, :], ACT.Copy
                                             ).then_inc(rounded.sem, 1)
                steps(act, body)
        self.node_records()

    def node_records(self):
        nc = self.nc
        with ExitStack() as s:
            def tmp(name, shape, dt=fp32):
                return s.enter_context(nc.sbuf_tensor(name, shape, dt))

            M = 2 * LO
            deg = [tmp(f"deg{k}", [HP, M]) for k in range(2)]
            cum, end, place, t_of, mask = (tmp(n, [HP, M]) for n in ("cum", "end", "place", "t_of", "mask"))
            ones = tmp("ones", [HP, M])
            alt = [tmp("alt0", [HP, M]), tmp("alt1", [HP, M])]
            tri = tmp("tri", [HP, HP])
            off = tmp("off", [HP, 1])
            record = tmp("record", [HP, M, MF])
            dinv = tmp("dinv", [HP, M])
            const, totals, offs, chain, made, stored = (self.sem(f"node_{n}") for n in
                                                        ("const", "totals", "offs", "chain", "made", "stored"))
            block = s.enter_context(nc.Block())

            @block.gpsimd
            def _(pool):
                nc.gpsimd.memset(tri[:, :], 1.0).then_inc(const, 1)
                pool.wait_ge(const, 1)
                nc.gpsimd.affine_select(out=tri[:, :], in_=tri[:, :], compare_op=ALU.is_gt, fill=0.0, base=0,
                                        pattern=[[1, HP]], channel_multiplier=-1).then_inc(const, 1)
                nc.gpsimd.iota(alt[0][:, :], pattern=[[0, 2], [1, LO]], base=2 * TROWS, channel_multiplier=0,
                               allow_small_or_imprecise_dtypes=True).then_inc(const, 1)
                nc.gpsimd.iota(alt[1][:, :], pattern=[[1, M]], base=0, channel_multiplier=M,
                               allow_small_or_imprecise_dtypes=True).then_inc(const, 1)
                nc.gpsimd.memset(record[:, :, :], 0.0).then_inc(const, 1)

            @block.tensor
            def _(pe):
                for k in range(2):
                    pe.wait_ge(totals, k + 1)
                    nc.tensor.matmul(self.bank[2 + k][0:HP, 0:1], tri[:, :], cum[:, M - 1:M], start=True,
                                     stop=True).then_inc(offs, 1)

            @block.vector
            def _(dve):
                link = Chain(dve, chain)
                link(nc.vector.memset(ones[:, :], 1.0))
                dve.wait_ge(const, 5)
                for k in range(2):
                    link(nc.vector.tensor_copy(deg[k][:, :], self.bank[k][0:HP, :]))
                    link(nc.vector.tensor_tensor_scan(out=cum[:, :], data0=ones[:, :], data1=deg[k][:, :], initial=0.0,
                                                      op0=ALU.mult, op1=ALU.add))
                    dve.sem_inc(totals, 1)
                    dve.wait_ge(offs, k + 1)
                    link(nc.vector.tensor_copy(off[:, :], self.bank[2 + k][0:HP, 0:1]))
                    link(nc.vector.tensor_scalar(end[:, :], cum[:, :], off[:, 0:1], -1.0, ALU.add, ALU.add))
                    link(nc.vector.tensor_scalar(t_of[:, :], end[:, :], float(-(EP // 2)), 1.0 / EP, ALU.add, ALU.mult))
                    link(nc.vector.tensor_scalar(t_of[:, :], t_of[:, :], MAGIC, None, ALU.add))
                    link(nc.vector.tensor_scalar(t_of[:, :], t_of[:, :], -MAGIC, None, ALU.add))
                    link(nc.vector.tensor_scalar(place[:, :], end[:, :], 1.0, float(NT), ALU.add, ALU.mult))
                    link(nc.vector.scalar_tensor_tensor(out=place[:, :], in0=t_of[:, :], scalar=float(1 - EP * NT),
                                                        in1=place[:, :], op0=ALU.mult, op1=ALU.add))
                    link(nc.vector.tensor_single_scalar(mask[:, :], deg[k][:, :], 0.5, op=ALU.is_gt))
                    link(nc.vector.scalar_tensor_tensor(out=place[:, :], in0=place[:, :], scalar=float(N * k),
                                                        in1=alt[k][:, :], op0=ALU.add, op1=ALU.subtract))
                    link(nc.vector.tensor_mul(place[:, :], place[:, :], mask[:, :]))
                    link(nc.vector.tensor_add(record[:, :, (F_L1, F_L2)[k]], place[:, :], alt[k][:, :]))
                    link(nc.vector.tensor_copy(record[:, :, (F_OUT, F_IN)[k]], deg[k][:, :]))
                    if k == 0:
                        link(nc.vector.scalar_tensor_tensor(out=record[:, :, F_SSTART], in0=end[:, :], scalar=1.0,
                                                            in1=deg[k][:, :], op0=ALU.add, op1=ALU.subtract))
                    else:
                        link(nc.vector.tensor_copy(record[:, :, F_DEND], end[:, :]))
                link(nc.vector.tensor_scalar(dinv[:, :], deg[1][:, :], 1.0, None, ALU.add))
                link(nc.vector.reciprocal(dinv[:, :], dinv[:, :]))
                dve.sem_inc(made, 1)

            @block.sync
            def _(sp):
                sp.wait_ge(made, 1)
                sp.dma_start(self.meta.rearrange("(p m) f -> p (m f)", p=HP),
                             record[:, :, :].rearrange("p m f -> p (m f)")).then_inc(stored, 16)
                sp.dma_start(self.dinv_n.rearrange("(p m) f -> p (m f)", p=HP), dinv[:, :]).then_inc(stored, 16)
                sp.wait_ge(stored, 32)

    def gather_rows(self, name, table, index, width, to, copy=None, clear=()):
        nc = self.nc
        picked, moved = (self.shared(f"gather_{n}") for n in ("picked", "moved"))
        stored, cleared = self.shared("gather_stored", True), self.shared("gather_cleared", True)
        filled = self.filled
        slot = [self.G[:, u * width:(u + 1) * width] for u in range(U)]
        with ExitStack() as s:
            if clear:
                zero = s.enter_context(nc.sbuf_tensor(f"{name}_zero", [P, ZJ * D], fp32))
                blank = self.sem(f"{name}_blank")
            block = s.enter_context(nc.Block())
            clears = 0
            if clear:
                @block.scalar
                def _(act):
                    nonlocal clears
                    act.wait_ge(blank, 1)
                    total = sum(-(-rows.shape[0] // parts // ZJ) for rows, parts in clear)
                    for rows, parts in clear:
                        n = rows.shape[0] // parts
                        v = rows.rearrange("(p n) d -> p (n d)", p=parts)
                        for j in range(0, n, ZJ):
                            m = min(ZJ, n - j)
                            act.wait_ge(moved.sem, moved.at + 2 + clears * 2 * NI // total)
                            act.dma_start(v[:, j * D:(j + m) * D], zero[0:parts, 0:m * D]).then_inc(cleared.sem, 16)
                            clears += 1
                    act.wait_ge(cleared.sem, cleared.at + 16 * clears)

            @block.gpsimd
            def _(pool):
                self.start(pool)
                with pool.Fori(0, NI) as n:
                    for h in range(2):
                        hold(pool, moved.sem, moved.at + n * 2 + h + 1, self.turns)
                        nc.gpsimd.tensor_copy(self.cur[:, h * H:(h + 1) * H],
                                              index[:, bass.ds(n * U + h * H, H)]).then_inc(picked.sem, 1)
                        hold(pool, picked.sem, picked.at + n * 2 + h + 1, self.turns)
                        for u in range(h * H, (h + 1) * H):
                            nc.gpsimd.indirect_dma_start(
                                out=slot[u], out_offset=None, in_=table,
                                in_offset=bass.IndirectOffsetOnAxis(ap=self.cur[:, u:u + 1], axis=0),
                            ).then_inc(filled[u].sem, 16)

            @block.vector
            def _(dve):
                if clear:
                    nc.vector.memset(zero[:, :], 0.0).then_inc(blank, 1)
                dve.sem_inc(moved.sem, 2)
                with dve.Fori(0, NI) as n:
                    for h in range(2):
                        for u in range(h * H, (h + 1) * H):
                            hold(dve, filled[u].sem, filled[u].at + n * 16 + 16, self.turns_dve)
                        nc.vector.tensor_copy(to[:, bass.ds((n * U + h * H) * width, H * width)],
                                              self.G[:, h * H * width:(h + 1) * H * width]).then_inc(moved.sem, 1)

            if copy is not None:
                @block.sync
                def _(sp):
                    sp.wait_ge(moved.sem, moved.at + 2 * NI + 2)
                    sp.dma_start(copy, to[:, :]).then_inc(stored.sem, 16)
                    sp.wait_ge(stored.sem, stored.at + 16)
        for u in range(U):
            filled[u].at += 16 * NI
        picked.at += 2 * NI
        moved.at += 2 * NI + 2
        stored.at += 16 * (copy is not None)
        cleared.at += 16 * clears

    def edge_mlp(self, s, block):
        nc, i = self.nc, self.i
        def tmp(name, shape, dt=fp32):
            return s.enter_context(nc.sbuf_tensor(name, shape, dt))

        def at_cols(start, size):
            return slice(start, start + size) if isinstance(start, int) else bass.ds(start, size)

        C = ED + 1
        w1 = tmp("w1a", [C, D])
        w2 = tmp("w2a", [D + 1, D])
        ea = tmp("ea", [P, 2, U * C])
        eat = tmp("eat", [C, U * P])
        hid = tmp("hid", [D + 1, U * P])
        weights, blank, in0, in1 = (self.sem(f"mlp_{n}") for n in ("weights", "blank", "in0", "in1"))
        turned, copied, hidden, rect, product, kept = (
            self.shared(f"mlp_{n}") for n in ("turned", "copied", "hidden", "rect", "product", "kept"))
        landed = (in0, in1)
        of = i["ea"]
        def steps(eng, body):
            with eng.Fori(0, NI // 2) as k:
                body(k * 2, 0)
                body(k * 2 + 1, 1)
            body(NI - 1, 0)

        @block.sync
        def _(sp):
            self.start(sp)
            with nc.allow_non_contiguous_dma(reason="weights are transposed once"):
                sp.dma_start(w1[0:ED, :], i["W1"].rearrange("c k -> k c")).then_inc(weights, 16)
                sp.dma_start(w1[ED:C, :], i["b1"].rearrange("(a c) -> a c", a=1)).then_inc(weights, 16)
                sp.dma_start(w2[0:D, :], i["W2"].rearrange("c k -> k c")).then_inc(weights, 16)
                sp.dma_start(w2[D:D + 1, :], i["b2"].rearrange("(a c) -> a c", a=1)).then_inc(weights, 16)
                sp.wait_ge(blank, 2)

                def body(n, b):
                    v = ea[:, b, :].rearrange("p (t c) -> p t c", c=C)
                    sp.wait_ge(turned.sem, turned.at + n * 2 + 2)
                    if isinstance(n, int):
                        first = n * U * EP
                        full = (E - first) // EP
                        sp.dma_start(v[1:P, 0:full, 0:ED], of[first:first + full * EP, :].rearrange(
                            "(t q) c -> q t c", q=EP)).then_inc(landed[b], 16)
                        sp.dma_start(v[1:REST + 1, full:full + 1, 0:ED], of[first + full * EP:E, :].rearrange(
                            "(t q) c -> q t c", t=1)).then_inc(landed[b], 16)
                    else:
                        sp.dma_start(v[1:P, :, 0:ED], of[bass.ds(n * (U * EP), U * EP), :].rearrange(
                            "(t q) c -> q t c", q=EP)).then_inc(landed[b], 16)
                steps(sp, body)

        @block.vector
        def _(dve):
            for b in range(2):
                nc.vector.memset(ea[:, b, :], 1.0).then_inc(blank, 1)
            nc.vector.memset(hid[D:D + 1, :], 1.0).then_inc(blank, 1)

        @block.tensor
        def _(pe):
            pe.sem_inc(turned.sem, 4)
            pe.wait_ge(weights, 64)
            pe.wait_ge(blank, 3)

            def body(n, b):
                pe.wait_ge(landed[b], 16 * (n // 2 + 2) if isinstance(n, int) else (n - b) * 8 + 16)
                for k in range(2):
                    pe.wait_ge(copied.sem, copied.at + n * 2)
                    for u in range(k * H, (k + 1) * H):
                        last = nc.tensor.transpose(self.bank[k][0:C, (u - k * H) * P:(u - k * H + 1) * P],
                                                   ea[:, b, u * C:(u + 1) * C], self.ident[:, :])
                    last.then_inc(turned.sem, 1)
                for k in range(2):
                    pe.wait_ge(copied.sem, copied.at + n * 2 + k + 1)
                    pe.wait_ge(rect.sem, rect.at + n * 2)
                    nc.tensor.matmul(self.bank[2 + k][0:D, :], w1[:, :], eat[:, k * H * P:(k + 1) * H * P],
                                     start=True, stop=True).then_inc(hidden.sem, 1)
                for k in range(2):
                    pe.wait_ge(rect.sem, rect.at + n * 2 + k + 1)
                    pe.wait_ge(kept.sem, kept.at + n * 2)
                    for u in range(k * H, (k + 1) * H):
                        last = nc.tensor.matmul(self.bank[4 + k][:, (u - k * H) * D:(u - k * H + 1) * D],
                                                hid[:, u * P:(u + 1) * P], w2[:, :], start=True, stop=True)
                    last.then_inc(product.sem, 1)
            steps(pe, body)

        @block.scalar
        def _(act):
            def body(n, b):
                for k in range(2):
                    act.wait_ge(turned.sem, turned.at + n * 2 + k + 5)
                    act.wait_ge(hidden.sem, hidden.at + n * 2)
                    nc.scalar.activation(eat[:, k * H * P:(k + 1) * H * P], self.bank[k][0:C, :],
                                         ACT.Copy).then_inc(copied.sem, 1)
                for k in range(2):
                    act.wait_ge(hidden.sem, hidden.at + n * 2 + k + 1)
                    act.wait_ge(product.sem, product.at + n * 2)
                    nc.scalar.activation(hid[0:D, k * H * P:(k + 1) * H * P], self.bank[2 + k][0:D, :],
                                         ACT.Relu).then_inc(rect.sem, 1)
                for k in range(2):
                    hold(act, product.sem, product.at + n * 2 + k + 1, self.turns_act)
                    nc.scalar.activation(self.T[:, at_cols((n * U + k * H) * D, H * D)],
                                         self.bank[4 + k][:, 0:H * D], ACT.Copy).then_inc(kept.sem, 1)
            steps(act, body)

    def edge_records(self):
        nc = self.nc
        with ExitStack() as s:
            def tmp(name, shape, dt=fp32):
                return s.enter_context(nc.sbuf_tensor(name, shape, dt))

            valid, rank, a, b, c, edge = (tmp(n, [P, NT]) for n in ("valid", "rank", "wa", "wb", "wc", "edge"))
            record, blank = tmp("edge_record", [P, NT, MF]), tmp("blank_record", [P, NT, MF])
            row = tmp("record_row", [P, NT], i32)
            ring = tmp("record_ring", [P, U * MF])
            ms = self.ms[:, :].rearrange("p (t f) -> p t f", f=MF)
            md = self.md[:, :].rearrange("p (t f) -> p t f", f=MF)
            const, roots, rooted, blanked, stored, chain, picked, moved = (
                self.sem(f"record_{n}") for n in ("const", "roots", "rooted", "blanked", "stored", "chain", "picked",
                                                  "moved"))
            sent = [self.shared(f"record_sent{h}", pool_dma=True) for h in range(2)]
            block = s.enter_context(nc.Block())

            @block.scalar
            def _(act):
                act.wait_ge(roots, 1)
                for x in (a, b, c):
                    nc.scalar.activation(x[:, :], x[:, :], ACT.Sqrt).then_inc(rooted, 1)

            @block.sync
            def _(sp):
                sp.wait_ge(blanked, 1)
                sp.dma_start(self.rec.rearrange("(p t) f -> p (t f)", p=P),
                             blank[:, :, :].rearrange("p t f -> p (t f)")).then_inc(stored, 16)
            self.edge_mlp(s, block)

            @block.vector
            def _(dve):
                v = nc.vector
                link = Chain(dve, chain)
                link(v.memset(blank[:, :, :], 0.0))
                link(v.memset(blank[:, :, R_KEY], PAD))
                link(v.memset(blank[:, :, R_L1], float(2 * TROWS)))
                link(v.memset(blank[:, :, R_TGT], float(BIG)))
                link(v.memset(record[:, :, :], 0.0))
                dve.sem_inc(blanked, 1)
                link(v.tensor_single_scalar(valid[:, :], self.src_f[:, :], float(N), op=ALU.is_lt))
                link(v.tensor_scalar(a[:, :], ms[:, :, F_IN], 1.0, None, ALU.add))
                link(v.tensor_scalar(b[:, :], md[:, :, F_IN], 1.0, None, ALU.add))
                link(v.tensor_scalar(c[:, :], ms[:, :, F_OUT], 1.0, None, ALU.max))
                link(v.tensor_scalar(rank[:, :], md[:, :, F_IN], 1.0, None, ALU.max))
                link(v.tensor_mul(c[:, :], c[:, :], rank[:, :]))
                link(v.reciprocal(self.self_c[:, :], b[:, :]))
                dve.sem_inc(roots, 1)
                link(v.tensor_add(rank[:, :], ms[:, :, F_SSTART], self.cnt[:, :]))
                dve.wait_ge(const, 1)
                link(v.tensor_tensor(out=edge[:, :], in0=edge[:, :], in1=md[:, :, F_DEND], op=ALU.is_equal))
                link(v.tensor_mul(edge[:, :], edge[:, :], valid[:, :]))
                link(v.scalar_tensor_tensor(out=edge[:, :], in0=self.key_d[:, :], scalar=float(-BIG), in1=edge[:, :],
                                            op0=ALU.add, op1=ALU.mult))
                link(v.tensor_scalar(self.tgt_d[:, :], edge[:, :], float(BIG), None, ALU.add))
                link(v.tensor_add(edge[:, :], ms[:, :, F_SSTART], ms[:, :, F_OUT]))
                link(v.tensor_scalar(edge[:, :], edge[:, :], -1.0, None, ALU.add))
                link(v.tensor_tensor(out=edge[:, :], in0=edge[:, :], in1=rank[:, :], op=ALU.is_equal))
                link(v.scalar_tensor_tensor(out=edge[:, :], in0=self.src_f[:, :], scalar=float(-BIG), in1=edge[:, :],
                                            op0=ALU.add, op1=ALU.mult))
                link(v.tensor_scalar(record[:, :, R_TGT], edge[:, :], float(BIG), None, ALU.add))
                link(v.tensor_copy(record[:, :, R_KEY], self.src_f[:, :]))
                link(v.tensor_copy(record[:, :, R_COL], self.key_d[:, :]))
                link(v.tensor_copy(record[:, :, R_L1], md[:, :, F_L1]))
                link(v.scalar_tensor_tensor(out=rank[:, :], in0=rank[:, :], scalar=float(1 - BIG), in1=valid[:, :],
                                            op0=ALU.add, op1=ALU.mult))
                link(v.tensor_scalar(row[:, :], rank[:, :], float(BIG), None, ALU.add))
                link(v.tensor_copy(self.l2[0][:, :], ms[:, :, F_L2]))
                link(v.tensor_single_scalar(edge[:, :], ms[:, :, F_L2], float(N), op=ALU.is_ge))
                link(v.scalar_tensor_tensor(out=self.l2[1][:, :], in0=edge[:, :], scalar=float(TROWS),
                                            in1=ms[:, :, F_L2], op0=ALU.mult, op1=ALU.add))
                dve.wait_ge(rooted, 3)
                for x in (a, b, c):
                    link(v.reciprocal(x[:, :], x[:, :]))
                link(v.tensor_mul(a[:, :], a[:, :], b[:, :]))
                link(v.tensor_mul(self.norm[:, :], a[:, :], valid[:, :]))
                link(v.scalar_tensor_tensor(out=record[:, :, R_W], in0=c[:, :], scalar=BETA, in1=valid[:, :],
                                            op0=ALU.mult, op1=ALU.mult))
                link(v.memset(self.norm[0:1, :], 1.0))
                link(v.memset(self.ones_d[:, :], 1.0))
                link(v.tensor_mul(self.ones_d[:, :], self.ones_d[:, :], valid[:, :]))
                link(v.memset(self.ones_d[0:1, :], 1.0))
                def fill_ring(n, h):
                    v.tensor_copy(ring[:, h * H * MF:(h + 1) * H * MF].rearrange("p (t f) -> p t f", f=MF),
                                  record[:, bass.ds(n * U + h * H, H), :]).then_inc(moved, 1)
                for h in range(2):
                    fill_ring(0, h)
                with dve.Fori(1, NI) as n:
                    for h in range(2):
                        hold(dve, sent[h].sem, sent[h].at + n * 16 * H, self.turns_dve)
                        fill_ring(n, h)

            @block.gpsimd
            def _(pool):
                nc.gpsimd.iota(edge[:, :], pattern=[[EP, NT]], base=-1, channel_multiplier=1,
                               allow_small_or_imprecise_dtypes=True).then_inc(const, 1)
                pool.wait_ge(stored, 16)
                with pool.Fori(0, NI) as n:
                    for h in range(2):
                        hold(pool, moved, n * 2 + h + 1, self.turns)
                        nc.gpsimd.tensor_copy(self.cur[:, h * H:(h + 1) * H],
                                              row[:, bass.ds(n * U + h * H, H)]).then_inc(picked, 1)
                        hold(pool, picked, n * 2 + h + 1, self.turns)
                        for u in range(h * H, (h + 1) * H):
                            nc.gpsimd.indirect_dma_start(
                                out=self.rec, out_offset=bass.IndirectOffsetOnAxis(ap=self.cur[:, u:u + 1], axis=0),
                                in_=ring[:, u * MF:(u + 1) * MF], in_offset=None, bounds_check=TROWS - 1,
                                oob_is_err=False).then_inc(sent[h].sem, 16)
                for h in range(2):
                    pool.wait_ge(sent[h].sem, sent[h].at + 16 * H * NI)

    def load_records(self, brow):
        nc = self.nc
        with ExitStack() as s:
            def tmp(name, shape, dt=fp32):
                return s.enter_context(nc.sbuf_tensor(name, shape, dt))

            got = tmp("records", [P, NT, MF])
            step = tmp("record_step", [P, NT])
            rowb = tmp("rowb_s", [CH, 2, P])
            landed, keyed, turned, made, stored, chain, spread = (
                self.sem(f"order_{n}") for n in ("landed", "keyed", "turned", "made", "stored", "chain", "spread"))
            tiles = bass.AP(self.rec.tensor, 0, [[MF, P], [EP * MF, NT], [1, MF]])
            block = s.enter_context(nc.Block())

            @block.scalar
            def _(act):
                act.dma_start(self.rows[:, :], brow.rearrange("t q -> (t q)").partition_broadcast(P)
                              ).then_inc(spread, 16)
                act.wait_ge(spread, 16)

            @block.sync
            def _(sp):
                sp.dma_start(got[:, :, :], tiles).then_inc(landed, 16)
                sp.wait_ge(made, 1)
                sp.dma_start(self.brow_s.rearrange("(c p) q -> p c q", c=2), rowb[:, :, :]).then_inc(stored, 16)
                sp.wait_ge(stored, 16)

            @block.vector
            def _(dve):
                v = nc.vector
                link = Chain(dve, chain)
                dve.wait_ge(landed, 16)
                link(v.tensor_copy(self.key_s[:, :], got[:, :, R_KEY]))
                dve.sem_inc(keyed, 1)
                link(v.tensor_copy(self.w_s[:, :], got[:, :, R_W]))
                link(v.memset(self.w_s[0:1, :], 1.0))
                link(v.tensor_copy(self.col_i[:, :], got[:, :, R_COL]))
                link(v.tensor_copy(self.tgt_s[:, :], got[:, :, R_TGT]))
                link(v.memset(self.tgt_s[0:1, :], BIG))
                link(v.tensor_copy(self.l1[0][:, :], got[:, :, R_L1]))
                link(v.tensor_single_scalar(step[:, :], got[:, :, R_L1], float(2 * TROWS), op=ALU.is_lt))
                link(v.scalar_tensor_tensor(out=self.l1[1][:, :], in0=step[:, :], scalar=float(TROWS),
                                            in1=got[:, :, R_L1], op0=ALU.mult, op1=ALU.add))
                dve.wait_ge(turned, 2)
                for c in range(2):
                    link(v.tensor_copy(rowb[:, c, :], self.bank[c][0:CH, 0:P]))
                link(v.tensor_copy(rowb[:, :, 0:1], rowb[:, :, P - 1:P]))
                dve.sem_inc(made, 1)

            @block.tensor
            def _(pe):
                pe.wait_ge(keyed, 1)
                for c in range(2):
                    nc.tensor.transpose(self.bank[c][0:CH, 0:P], self.key_s[:, c * CH:(c + 1) * CH],
                                        self.ident[:, :]).then_inc(turned, 1)

    def passes(self, name, mode, table=None):
        nc = self.nc
        K = {"mul": 1, "plain": 1, "power": K1, "smooth": K2}[mode]
        tables = {"power": self.tab1, "smooth": self.tab2}.get(mode)
        table_at = N if mode == "smooth" else 0
        first = {"mul": self.i["x"], "plain": table, "power": self.x1,
                 "smooth": self.tab2}[mode]
        index0 = self.col_i if mode == "power" else self.src_i
        later = self.l1 if mode == "power" else self.l2
        agg, target = (self.agg_s, self.tgt_s) if mode == "power" else (self.agg_d, self.tgt_d)
        key = self.key_s if mode == "power" else self.key_d
        weight = {"mul": self.ones_d, "power": self.w_s}.get(mode, self.norm)
        update, smooth = mode == "power", mode == "smooth"
        sig = {n: self.shared(f"pass_{n}") for n in ("picked", "placed", "multiplied", "carry_made", "carried", "gated",
                                                     "emptied", "updated0", "updated1", "linked", "selfed")}
        stored = [self.shared(f"pass_stored{h}", True) for h in range(2)]
        sent = [self.shared(f"pass_sent{h}", pool_dma=True) for h in range(2)]
        landed = [self.shared(f"pass_landed{h}", True) for h in range(2)]
        picked, placed, multiplied, carry_made, carried, gated, emptied, linked, selfed = (
            sig[n] for n in ("picked", "placed", "multiplied", "carry_made", "carried", "gated", "emptied", "linked", "selfed"))
        updated = [sig["updated0"], sig["updated1"]]
        filled = self.filled
        O, G = self.O, self.G
        U, H, NI = UP, UP // 2, NT // UP
        main, carry = self.bank[0:H], self.bank[H:H + 2]
        HD = H * D
        AHEAD = 2

        def rounds(eng, one):
            one(0, 0, True, K == 1)
            if K > 2:
                with eng.Fori(0, (K - 2) // 2) as k:
                    one(k * 2 + 1, 1, False, False)
                    one(k * 2 + 2, 0, False, False)
            if K > 1:
                one(K - 1, (K - 1) % 2, False, True)

        def at_cols(start, size):
            return slice(start, start + size) if isinstance(start, int) else bass.ds(start, size)

        with ExitStack() as s:
            def tmp(n, shape, dt=fp32):
                return s.enter_context(nc.sbuf_tensor(f"{name}_{n}", shape, dt))

            S = tmp("S", [P, U * P])
            if mode == "smooth":
                xs, own = tmp("xs", [P, U * D]), tmp("own", [P, H * D])
                share_x = [tmp(f"share_x{k}", [P, P]) for k in range(2)]
            block = s.enter_context(nc.Block())

            @block.gpsimd
            def _(pool):
                self.start(pool)

                def one(p, par, is_first, is_last):
                    source = first if is_first else tables
                    index = index0 if is_first else later[(par + 1) % 2]
                    if not is_first:
                        for h in range(2):
                            hold(pool, stored[h].sem, stored[h].at + p * 16 * NI, self.turns)

                    def pick(n, h):
                        hold(pool, multiplied.sem, multiplied.at + (p * NI + n) * U + (h * H + H), self.turns)
                        nc.gpsimd.tensor_copy(self.cur[:, h * H:(h + 1) * H],
                                              index[:, at_cols(n * U + h * H, H)]).then_inc(picked.sem, 1)

                    def gather(n, h, ends=False):
                        hold(pool, picked.sem, picked.at + (p * NI + n) * 2 + h + 1, self.turns)
                        for u in range(h * H, (h + 1) * H):
                            if u == (h + 1) * H - 1 and not ends:
                                pick(n + h, 1 - h)
                            nc.gpsimd.indirect_dma_start(
                                out=G[:, u * D:(u + 1) * D], out_offset=None, in_=source,
                                in_offset=bass.IndirectOffsetOnAxis(ap=self.cur[:, u:u + 1], axis=0),
                            ).then_inc(filled[u].sem, 16)

                    def scatter(n, h):
                        if update:
                            hold(pool, updated[h].sem, updated[h].at + p * NI + n + 1, self.turns)
                        else:
                            hold(pool, emptied.sem, emptied.at + H + (p * NI + n) * U + (h * H + H), self.turns)
                        if not (isinstance(n, int) and n == 0):
                            hold(pool, sent[h].sem, sent[h].at + n * 16 * H, self.turns)
                        nc.gpsimd.tensor_copy(self.cur[:, U + h * H:U + (h + 1) * H],
                                              target[:, at_cols(n * U + h * H, H)]).then_inc(placed.sem, 1)
                        hold(pool, placed.sem, placed.at + n * 2 + h + 1, self.turns)
                        for u in range(h * H, (h + 1) * H):
                            nc.gpsimd.indirect_dma_start(
                                out=agg, out_offset=bass.IndirectOffsetOnAxis(ap=self.cur[:, U + u:U + u + 1], axis=0),
                                in_=O[:, u * D:(u + 1) * D], in_offset=None, bounds_check=N - 1, oob_is_err=False,
                            ).then_inc(sent[h].sem, 16)

                    pick(0, 0)
                    if not is_last:
                        with pool.Fori(0, NI - 1) as n:
                            for h in range(2):
                                gather(n, h)
                        gather(NI - 1, 0)
                        gather(NI - 1, 1, ends=True)
                    else:
                        for h in range(2):
                            gather(0, h)
                        for h in range(2):
                            gather(1, h)
                            scatter(0, h)
                        with pool.Fori(1, NI - 2) as n:
                            for h in range(2):
                                gather(n + 1, h)
                                scatter(n, h)
                        for h in range(2):
                            gather(NI - 1, h, ends=h == 1)
                            scatter(NI - 2, h)
                        for h in range(2):
                            scatter(NI - 1, h)
                        for h in range(2):
                            pool.wait_ge(sent[h].sem, sent[h].at + 16 * H * NI)
                rounds(pool, one)

            @block.tensor
            def _(pe):
                pe.sem_inc(multiplied.sem, U)
                if smooth:
                    pe.wait_ge(linked.sem, linked.at + 3)

                def one(p, par, is_first, is_last):
                    with pe.Fori(0, NI) as n:
                        for u in range(U):
                            tile = (p * NI + n) * U + u
                            pe.wait_ge(carried.sem, carried.at + tile + 1)
                            nc.tensor.matmul(carry[u % 2][0:1, 0:D], S[:, u * P:u * P + 1],
                                             G[:, u * D:(u + 1) * D], start=True, stop=True).then_inc(carry_made.sem, 1)
                            pe.wait_ge(emptied.sem, emptied.at + tile + 1)
                            if smooth:
                                pe.wait_ge(selfed.sem, selfed.at + tile + 1)
                                nc.tensor.matmul(main[u % H][:, 0:D], self.ident[:, :],
                                                 own[:, u % H * D:(u % H + 1) * D], start=True, stop=False)
                                pe.wait_ge(landed[u // H].sem, landed[u // H].at + (p * NI + n) * 16 + 16)
                                nc.tensor.matmul(main[u % H][:, 0:D], share_x[is_last][:, :],
                                                 xs[:, u * D:(u + 1) * D], start=False, stop=False)
                            nc.tensor.matmul(main[u % H][:, 0:D], S[:, u * P:(u + 1) * P],
                                             G[:, u * D:(u + 1) * D], start=not smooth, stop=True
                                             ).then_inc(multiplied.sem, 1)
                rounds(pe, one)

            @block.scalar
            def _(act):
                act.sem_inc(emptied.sem, H)

                def fetch(n, h):
                    act.dma_start(xs[:, h * HD:(h + 1) * HD], self.xp[:, at_cols((n * U + h * H) * D, HD)]
                                  ).then_inc(landed[h].sem, 16)

                def of_their_own(p, n, u):
                    t = n * U + u
                    act.wait_ge(multiplied.sem, multiplied.at + p * NT + U - H + t + 1)
                    act.sem_inc(self.turns_act, 1)
                    nc.scalar.activation(own[:, u % H * D:(u % H + 1) * D], self.T[:, at_cols(t * D, D)],
                                         ACT.Copy, scale=self.self_c[:, at_cols(t, 1)]).then_inc(selfed.sem, 1)

                def one(p, par, is_first, is_last):
                    def half_of(n, h, follows):
                        step = p * NI + n
                        if update:
                            act.wait_ge(updated[h].sem, updated[h].at + step)
                            act.sem_inc(self.turns_act, 1)
                        if mode == "power" and not is_last:
                            act.wait_ge(stored[h].sem, stored[h].at + step * 16)
                            act.sem_inc(self.turns_act, 1)
                        if mode == "power" and is_last:
                            act.wait_ge(stored[h].sem, stored[h].at + (K - 1) * NI * 16)
                        if is_last and not (isinstance(n, int) and n == 0):
                            act.wait_ge(sent[h].sem, sent[h].at + n * 16 * H)
                            act.sem_inc(self.turns_act, 1)
                        for u in range(h * H, (h + 1) * H):
                            if smooth and not (isinstance(n, int) and n * U + u + AHEAD >= NT):
                                v = u + AHEAD
                                of_their_own(p, n + v // U, v % U)
                            act.wait_ge(multiplied.sem, multiplied.at + U + step * U + u + 1)
                            if smooth and not is_last:
                                act.sem_inc(self.turns_act, 1)
                                to = self.T[:, at_cols((n * U + u) * D, D)]
                            else:
                                to = O[:, u * D:(u + 1) * D]
                            nc.scalar.activation(to, main[u % H][:, 0:D], ACT.Copy, scale=0.9 if smooth else 1.0
                                                 ).then_inc(emptied.sem, 1)
                        if smooth and follows is not None:
                            fetch(follows, h)
                    if smooth:
                        act.wait_ge(emptied.sem, emptied.at + H + p * NT)
                        for u in range(AHEAD):
                            of_their_own(p, 0, u)
                    for h in range(2):
                        half_of(0, h, 1)
                    with act.Fori(1, NI - 1) as n:
                        for h in range(2):
                            half_of(n, h, n + 1)
                    for h in range(2):
                        half_of(NI - 1, h, None if is_last else 0)
                if smooth:
                    for h in range(2):
                        fetch(0, h)
                rounds(act, one)

            @block.vector
            def _(dve):
                nc.vector.memset(carry[1][0:1, 0:D], 0.0).then_inc(linked.sem, 1)
                dve.wait_ge(linked.sem, linked.at + 1)
                if smooth:
                    for k, share in enumerate((0.1 / 0.9, -1.0)):
                        nc.vector.tensor_single_scalar(share_x[k][:, :], self.ident[:, :], share, op=ALU.mult
                                                       ).then_inc(linked.sem, 1)

                def one(p, par, is_first, is_last):
                    def build(n, u):
                        t = n * U + u
                        dve.wait_ge(multiplied.sem, multiplied.at + p * NT + t + 1)
                        nc.vector.tensor_scalar(S[:, u * P:(u + 1) * P], self.rows[:, at_cols(t * P, P)],
                                                key[:, at_cols(t, 1)], weight[:, at_cols(t, 1)],
                                                ALU.is_equal, ALU.mult)

                    def carry_on(n, u):
                        step = p * NI + n
                        tile = step * U + u
                        slot = G[:, u * D:(u + 1) * D]
                        dve.wait_ge(filled[u].sem, filled[u].at + step * 16 + 16)
                        if mode == "mul":
                            nc.vector.tensor_mul(slot, slot, self.T[:, at_cols((n * U + u) * D, D)]
                                                 ).then_inc(gated.sem, 1)
                            dve.wait_ge(gated.sem, gated.at + tile + 1)
                        dve.wait_ge(carry_made.sem, carry_made.at + tile)
                        nc.vector.tensor_copy(slot[0:1, :], carry[(u + 1) % 2][0:1, 0:D]).then_inc(carried.sem, 1)

                    def renew(n, h):
                        step = p * NI + n
                        half = O[:, h * HD:(h + 1) * HD]
                        there = self.T[:, at_cols((n * U + h * H) * D, HD)]
                        if mode == "power":
                            dve.wait_ge(emptied.sem, emptied.at + H + step * U + (h + 1) * H)
                            if is_first:
                                dve.sem_inc(self.turns_dve, 1)
                                nc.vector.tensor_copy(there, half).then_inc(updated[h].sem, 1)
                            elif is_last:
                                nc.vector.scalar_tensor_tensor(out=half, in0=there, scalar=0.1, in1=half,
                                                               op0=ALU.mult, op1=ALU.add).then_inc(updated[h].sem, 1)
                            else:
                                nc.vector.tensor_add(there, there, half).then_inc(updated[h].sem, 1)

                    def step_of(n, begins, ends):
                        for u in range(H):
                            carry_on(n, u)
                            build(n, H + u)
                        if not begins:
                            renew(n - 1, 1)
                        for u in range(H):
                            carry_on(n, H + u)
                            if not ends:
                                build(n + 1, u)
                        renew(n, 0)
                        if ends:
                            renew(n, 1)
                    for u in range(H):
                        build(0, u)
                    step_of(0, True, False)
                    with dve.Fori(1, NI - 1) as n:
                        step_of(n, False, False)
                    step_of(NI - 1, False, True)
                rounds(dve, one)

            if K > 1:
                @block.sync
                def _(sp):
                    def one(p, par, is_first, is_last):
                        places = None if is_last else tables[table_at + par * TROWS:table_at + (par + 1) * TROWS, :].rearrange(
                            "(p t) d -> p (t d)", p=P)
                        with sp.Fori(0, NI) as n:
                            step = p * NI + n
                            for h in range(2):
                                if is_last:
                                    continue
                                cols = bass.ds((n * U + h * H) * D, HD)
                                if mode == "power":
                                    sp.wait_ge(emptied.sem, emptied.at + H + step * U + (h + 1) * H)
                                    sp.dma_start(places[:, cols], O[:, h * HD:(h + 1) * HD]
                                                 ).then_inc(stored[h].sem, 16)
                                else:
                                    sp.wait_ge(emptied.sem, emptied.at + H + step * U + (h + 1) * H)
                                    sp.sem_inc(self.turns_sp, 1)
                                    sp.dma_start(places[:, cols], self.T[:, cols]).then_inc(stored[h].sem, 16)
                    rounds(sp, one)
                    for h in range(2):
                        sp.wait_ge(stored[h].sem, stored[h].at + (K - 1) * 16 * NI)
        tiles = K * NT
        for f in filled:
            f.at += K * NI * 16
        picked.at += K * 2 * NI
        placed.at += 2 * NI
        multiplied.at += tiles + U
        carry_made.at += tiles
        carried.at += tiles
        emptied.at += tiles + H
        gated.at += tiles * (mode == "mul")
        linked.at += 1 + 2 * smooth
        selfed.at += tiles * smooth
        for h in range(2):
            updated[h].at += K * NI * update
            stored[h].at += (K - 1) * 16 * NI
            sent[h].at += 16 * H * NI
            landed[h].at += K * NI * 16 * (mode == "smooth")

    def dense(self, kind, brow=None):
        nc, i = self.nc, self.i
        W = J * D
        B = 4
        R4 = 4
        x2 = self.tab2[0:N, :]
        first = {"d0": i["x"], "d1": self.x1, "d2": x2, "d3": self.z1, "d4": self.z2}[kind]
        agg = self.agg_s if kind == "d1" else self.agg_d
        norm_to = {"d0": self.x1, "d1": x2, "d2": self.x3, "d4": self.out}.get(kind)
        product_to = {"d2": self.z1, "d3": self.z2}.get(kind)
        normed = norm_to is not None
        conv = kind in ("d3", "d4")
        loads = 2
        names = ("read", "turned", "copied", "product", "summed", "centred", "squared", "spread", "rooted", "inverted", "divided",
                 "shifted", "scaled", "active", "kept", "inner", "averaged", "added", "totalled")
        sig = {n: self.shared(f"dense_{n}") for n in names}
        read, turned, copied, product, summed, centred, squared, spread, rooted, inverted, divided, shifted, scaled, active, kept, inner, averaged, added, totalled = (
            sig[n] for n in names)
        landed = [self.shared(f"dense_landed{b}", True) for b in range(B)]
        stored = [self.shared(f"dense_stored{b}", True) for b in range(B)]
        x3_there = [self.shared(f"dense_x3_{b}", True) for b in range(B)]
        late = 2 if kind == "d4" else 0
        zstored = [self.shared(f"dense_zstored{b}", True) for b in range(B)]
        wts = self.shared("dense_weights", True)
        keys = self.shared("dense_keys", True)
        const = self.shared("dense_const")
        rows = lambda t: t.rearrange("(p j) d -> p (j d)", p=NP_)
        LMAX = 8

        def run(eng, parts):
            def turn(it, j):
                for lag, fn in parts:
                    if isinstance(it, int) and not 0 <= it - lag < NG:
                        continue
                    fn(it - lag, (j - lag) % B)
            for it in range(LMAX):
                turn(it, it)
            loops = (NG - LMAX) // B
            with eng.Fori(0, loops) as k:
                for j in range(B):
                    turn(k * B + (LMAX + j), LMAX + j)
            for it in range(LMAX + loops * B, NG + LMAX):
                turn(it, it)

        with ExitStack() as s:
            def tmp(n, shape, dt=fp32):
                return s.enter_context(nc.sbuf_tensor(f"{kind}_{n}", shape, dt))

            X, A, Rr = tmp("X", [NP_, B * W]), tmp("A", [NP_, B * W]), tmp("R", [NP_, B * W])
            if normed:
                C, Q = tmp("C", [NP_, B * W]), tmp("Q", [NP_, B * W])
            mean, var, std, inv = (tmp(n, [NP_, B * J]) for n in ("mean", "var", "std", "inv"))
            eps = tmp("eps", [P, 1])
            if kind == "d0":
                xt = tmp("xt", [D + 2, 2 * J * NP_])
                at_ = tmp("at", [D, 2 * J * NP_])
                wa, wb = tmp("wa", [D + 2, D]), tmp("wb", [D, D])
            if product_to is not None:
                xt = tmp("xt", [D, 2 * J * NP_])
                wa = tmp("wa", [D, D])
                Z = tmp("Z", [NP_, B * W])
            if conv:
                dinv = tmp("dinv", [NP_, NJ])
                bias, slope = tmp("bias", [NP_, D]), tmp("slope", [NP_, D])
            if kind == "d4":
                X3 = tmp("X3", [NP_, B * W])
            n_w = {"d0": 4, "d1": 0, "d2": 1, "d3": 4, "d4": 3}[kind]

            def v2(x, b):
                return x[:, b * W:(b + 1) * W]

            def v3(x, b):
                return v2(x, b).rearrange("p (j d) -> p j d", d=D)

            def per_row(x, b):
                return x[:, b * J:(b + 1) * J].unsqueeze(2).to_broadcast([NP_, J, D])

            def per_feature(x):
                return x[:, :].unsqueeze(1).to_broadcast([NP_, J, D])

            def data(sg, g, b, m=1):
                return sg.at + (g - b) * (16 // B) * m + 16 * m

            def before(sg, g, b, m=1):
                return sg.at + (g - b) * (16 // B) * m

            if True:
                def load(g, b):
                    eng = nc.sync
                    hold(eng, read.sem, read.at + g + 1, self.turns_sp)
                    cols = bass.ds(g * W, W) if not isinstance(g, int) else slice(g * W, (g + 1) * W)
                    eng.dma_start(v2(X, b), rows(first)[:, cols]).then_inc(landed[b].sem, 16)
                    eng.dma_start(v2(A, b), rows(agg)[:, cols]).then_inc(landed[b].sem, 16)

                def load_keys(g, b):
                    M = NT // NG
                    cols = bass.ds(g * (M * P), M * P) if not isinstance(g, int) else slice(g * M * P, (g + 1) * M * P)
                    nc.sync.dma_start(self.rows[:, cols], brow.rearrange("t q -> (t q)")[cols].partition_broadcast(P)
                                      ).then_inc(keys.sem, 16)

                def load_x3(g, b):
                    hold(nc.sync, added.sem, added.at + g + 1, self.turns_sp)
                    cols = bass.ds(g * W, W) if not isinstance(g, int) else slice(g * W, (g + 1) * W)
                    nc.sync.dma_start(v2(X3, b), rows(self.x3)[:, cols]).then_inc(x3_there[b].sem, 16)

                def store(g, b):
                    eng = nc.sync
                    hold(eng, divided.sem, divided.at + g + 1 + B, self.turns_sp)
                    cols = bass.ds(g * W, W) if not isinstance(g, int) else slice(g * W, (g + 1) * W)
                    eng.dma_start(rows(norm_to)[:, cols], v2(C, b)).then_inc(stored[b].sem, 16)

                def store_z(g, b):
                    eng = nc.sync
                    hold(eng, kept.sem, kept.at + g * 2 + 2 + 4, self.turns_sp)
                    cols = bass.ds(g * W, W) if not isinstance(g, int) else slice(g * W, (g + 1) * W)
                    eng.dma_start(rows(product_to)[:, cols], v2(Z, b)).then_inc(zstored[b].sem, 16)

            block = s.enter_context(nc.Block())

            @block.sync
            def _(sp):
                n = 0
                with nc.allow_non_contiguous_dma(reason="weights are transposed once"):
                    def weight(to, of):
                        nonlocal n
                        sp.dma_start(to, of).then_inc(wts.sem, 16)
                        n += 1
                    if kind == "d0":
                        weight(wa[0:D, :], i["Ws"].rearrange("c k -> k c"))
                        weight(wa[D:D + 1, :], i["bs"].rearrange("(a c) -> a c", a=1))
                        weight(wa[D + 1:D + 2, :], i["bn"].rearrange("(a c) -> a c", a=1))
                        weight(wb[:, :], i["Wn"].rearrange("c k -> k c"))
                    if kind == "d2":
                        weight(wa[:, :], i["V1"])
                    if kind == "d3":
                        weight(wa[:, :], i["V2"])
                    if conv:
                        weight(dinv[:, :], self.dinv_n[0:N, :].rearrange("(p j) a -> p (j a)", p=NP_))
                        weight(bias[:, :], i["c1" if kind == "d3" else "c2"].partition_broadcast(NP_))
                        weight(slope[:, :], i["prelu_a"].partition_broadcast(NP_))
                assert n == n_w
                parts = [(0, load)]
                if brow is not None:
                    parts.append((1, load_keys))
                if kind == "d4":
                    parts.append((1, load_x3))
                if normed:
                    parts.append((6 + late, store))
                if product_to is not None:
                    parts.append((8 if kind == "d2" else 5, store_z))
                run(sp, parts)
                if brow is not None:
                    sp.wait_ge(keys.sem, keys.at + 16 * NG)
                for b in range(B):
                    groups = len(range(b, NG, B))
                    if normed:
                        sp.wait_ge(stored[b].sem, stored[b].at + 16 * groups)
                    if product_to is not None:
                        sp.wait_ge(zstored[b].sem, zstored[b].at + 16 * groups)

            mm_from = {"d0": 2, "d2": 7, "d3": 4}.get(kind)

            @block.tensor
            def _(pe):
                if mm_from is None:
                    return
                pe.sem_inc(product.sem, 2)
                pe.wait_ge(wts.sem, wts.at + 16 * n_w)
                pe.wait_ge(const.sem, const.at + 2)

                def turn(g, b):
                    if kind == "d0":
                        pe.wait_ge(landed[b].sem, data(landed[b], g, b, 2))
                        sources = (X, A)
                    elif kind == "d2":
                        pe.wait_ge(divided.sem, divided.at + g + 1 + B)
                        sources = (C,)
                    else:
                        pe.wait_ge(active.sem, active.at + g + 1)
                        sources = (Rr,)
                    pe.wait_ge(copied.sem, copied.at + g * 2 * len(sources) + 2 * B)
                    k = 0
                    for half in range(2):
                        for src in sources:
                            for j in range(R4):
                                c0 = b * W + (half * R4 + j) * D
                                last = nc.tensor.transpose(self.bank[k][0:D, j * NP_:(j + 1) * NP_],
                                                           src[:, c0:c0 + D], self.ident[0:NP_, 0:NP_])
                            last.then_inc(turned.sem, 1)
                            k += 1

                def mult(g, b):
                    n_src = 2 if kind == "d0" else 1
                    if kind == "d0":
                        pe.wait_ge(read.sem, read.at + g + B - 1)
                    else:
                        pe.wait_ge(kept.sem, kept.at + g * 2 + 2)
                    b2 = b % 2
                    for half in range(2):
                        pe.wait_ge(copied.sem, copied.at + (g * 2 + half + 1) * n_src + 2 * B)
                        for j in range(R4):
                            r = (b2 * J + half * R4 + j) * NP_
                            o = self.bank[4 + b2 * 2 + half][0:NP_, j * D:(j + 1) * D]
                            if kind == "d0":
                                nc.tensor.matmul(o, xt[:, r:r + NP_], wa[:, :], start=True, stop=False)
                                last = nc.tensor.matmul(o, at_[:, r:r + NP_], wb[:, :], start=False, stop=True)
                            else:
                                last = nc.tensor.matmul(o, xt[:, r:r + NP_], wa[:, :], start=True, stop=True)
                    last.then_inc(product.sem, 1)
                run(pe, [(mm_from, turn), (mm_from, mult)])

            @block.scalar
            def _(act):
                def copy(g, b):
                    b2 = b % 2
                    act.wait_ge(product.sem, product.at + g + 1)
                    k = 0
                    n_src = 2 if kind == "d0" else 1
                    for half in range(2):
                        for to in ((xt, at_) if kind == "d0" else (xt,)):
                            act.wait_ge(turned.sem, turned.at + g * 2 * n_src + k + 1)
                            c0 = (b2 * J + half * R4) * NP_
                            nc.scalar.activation(to[0:D, c0:c0 + R4 * NP_], self.bank[k][0:D, 0:R4 * NP_], ACT.Copy
                                                 ).then_inc(copied.sem, 1)
                            k += 1

                def square(g, b):
                    act.wait_ge(centred.sem, centred.at + g + 1 + B)
                    act.wait_ge(spread.sem, spread.at + g + 1)
                    nc.scalar.activation(v2(Q, b), v2(C, b), ACT.Square).then_inc(squared.sem, 1)

                def root(g, b):
                    act.wait_ge(spread.sem, spread.at + g + 1 + B)
                    act.wait_ge(inverted.sem, inverted.at + g + 1)
                    nc.scalar.activation(std[:, b * J:(b + 1) * J], var[:, b * J:(b + 1) * J], ACT.Sqrt,
                                         bias=eps[0:NP_, :], scale=1.0 / D).then_inc(rooted.sem, 1)

                def scale_agg(g, b):
                    act.wait_ge(landed[b].sem, data(landed[b], g, b, 2))
                    nc.scalar.activation(v2(A, b), v2(A, b), ACT.Copy, scale=1.0 / THETA).then_inc(scaled.sem, 1)

                def keep(g, b):
                    b2 = b % 2
                    act.wait_ge(product.sem, product.at + g + 1 + 2)
                    act.wait_ge(zstored[b].sem, before(zstored[b], g, b))
                    for half in range(2):
                        c0 = b * W + half * R4 * D
                        nc.scalar.activation(Z[:, c0:c0 + R4 * D], self.bank[4 + b2 * 2 + half][0:NP_, 0:R4 * D],
                                             ACT.Copy).then_inc(kept.sem, 1)

                def average(g, b):
                    hold(act, landed[b].sem, data(landed[b], g, b, loads), self.turns_act)
                    for j in range(J):
                        c0 = b * W + j * D
                        col = bass.ds(g * J + j, 1) if not isinstance(g, int) else slice(g * J + j, g * J + j + 1)
                        last = nc.scalar.activation(X[:, c0:c0 + D], X[:, c0:c0 + D], ACT.Copy, scale=dinv[:, col])
                    last.then_inc(averaged.sem, 1)
                if kind == "d4":
                    act.wait_ge(wts.sem, wts.at + 16 * n_w)
                act.wait_ge(const.sem, const.at + 2)
                act.sem_inc(copied.sem, 2 * B)
                act.sem_inc(kept.sem, 4)
                act.sem_inc(rooted.sem, B)
                parts = [(5 + late, root), (4 + late, square)] if normed else []
                if kind == "d4":
                    parts.append((2, average))
                if product_to is not None:
                    parts.append((mm_from + 1, keep))
                if mm_from is not None:
                    parts.append((mm_from, copy))
                if kind == "d1":
                    parts.append((2, scale_agg))
                run(act, parts)

            @block.vector
            def _(dve):
                nc.vector.memset(eps[:, :], 1e-5).then_inc(const.sem, 1)
                if kind == "d0":
                    nc.vector.memset(xt[D:D + 2, :], 1.0).then_inc(const.sem, 1)
                else:
                    dve.sem_inc(const.sem, 1)
                dve.sem_inc(read.sem, B)
                dve.sem_inc(spread.sem, B)
                dve.sem_inc(inverted.sem, B)
                if conv:
                    dve.wait_ge(wts.sem, wts.at + 16 * n_w)
                steps = {"d0": 3, "d1": 2, "d2": 2, "d3": 2, "d4": 2}[kind]

                def residual(g, b):
                    done = [0]

                    def link(ins):
                        done[0] += 1
                        ins.then_inc(inner.sem, 1)
                        dve.wait_ge(inner.sem, inner.at + g * steps + done[0])
                    if normed:
                        dve.wait_ge(centred.sem, centred.at + g + 1)
                    else:
                        dve.wait_ge(copied.sem, copied.at + g * 2 + 2)
                    dve.wait_ge(landed[b].sem, data(landed[b], g, b, loads))
                    v = nc.vector
                    if kind == "d0":
                        dve.wait_ge(product.sem, product.at + g + 1 + 2)
                        for half in range(2):
                            c0 = b * W + half * R4 * D
                            link(v.scalar_tensor_tensor(out=Rr[:, c0:c0 + R4 * D],
                                                        in0=self.bank[4 + (b % 2) * 2 + half][0:NP_, 0:R4 * D],
                                                        scalar=0.0, in1=X[:, c0:c0 + R4 * D], op0=ALU.max, op1=ALU.add))
                    elif kind == "d1":
                        dve.wait_ge(scaled.sem, scaled.at + g + 1)
                        link(v.scalar_tensor_tensor(out=v2(Rr, b), in0=v2(X, b), scalar=1.0 + 0.1 / THETA,
                                                    in1=v2(A, b), op0=ALU.mult, op1=ALU.add))
                    elif kind == "d2":
                        link(v.scalar_tensor_tensor(out=v2(Rr, b), in0=v2(X, b), scalar=2.0, in1=v2(A, b),
                                                    op0=ALU.mult, op1=ALU.add))
                    else:
                        dve.wait_ge(shifted.sem, shifted.at + g + 1)
                        dve.wait_ge(averaged.sem, averaged.at + g + 1)
                        link(v.tensor_add(v2(Rr, b), v2(X, b), v2(A, b)))
                        link(v.scalar_tensor_tensor(out=v3(A, b), in0=v3(Rr, b), scalar=0.0, in1=per_feature(slope),
                                                    op0=ALU.min, op1=ALU.mult))
                        last = v.scalar_tensor_tensor(out=v2(Rr, b), in0=v2(Rr, b), scalar=0.0, in1=v2(A, b),
                                                      op0=ALU.max, op1=ALU.add)
                        last.then_inc(active.sem, 1)
                        dve.wait_ge(active.sem, active.at + g + 1)
                        dve.sem_inc(read.sem, 1)
                        return
                    dve.sem_inc(read.sem, 1)
                    average_of(g, b, link)

                def x3_added(g, b):
                    def link(ins):
                        ins.then_inc(totalled.sem, 1)
                        dve.wait_ge(totalled.sem, totalled.at + g + 1)
                    dve.wait_ge(added.sem, added.at + g + 1 + B)
                    average_of(g, b, link)

                def average_of(g, b, link):
                    v = nc.vector
                    link(v.tensor_reduce(out=mean[:, b * J:(b + 1) * J], in_=v3(Rr, b), axis=AXX, op=ALU.add))
                    v.tensor_single_scalar(mean[:, b * J:(b + 1) * J], mean[:, b * J:(b + 1) * J], -1.0 / D,
                                           op=ALU.mult).then_inc(summed.sem, 1)

                def variance(g, b):
                    dve.wait_ge(squared.sem, squared.at + g + 1)
                    dve.wait_ge(rooted.sem, rooted.at + g + 1)
                    nc.vector.tensor_reduce(out=var[:, b * J:(b + 1) * J], in_=v3(Q, b), axis=AXX, op=ALU.add
                                            ).then_inc(spread.sem, 1)
                def invert(g, b):
                    dve.wait_ge(rooted.sem, rooted.at + g + 1 + B)
                    dve.wait_ge(divided.sem, divided.at + g + 1)
                    nc.vector.reciprocal(inv[:, b * J:(b + 1) * J], std[:, b * J:(b + 1) * J]).then_inc(inverted.sem, 1)
                parts = [(6 + late, invert), (5 + late, variance)] if normed else []
                if kind == "d4":
                    parts.append((5, x3_added))
                run(dve, parts + [(3, residual)])

            @block.gpsimd
            def _(pool):
                self.start(pool)
                if normed:
                    pool.sem_inc(centred.sem, B)
                    pool.sem_inc(divided.sem, B)
                if kind == "d4":
                    pool.sem_inc(added.sem, B)
                if conv:
                    pool.wait_ge(wts.sem, wts.at + 16 * n_w)

                def shift(g, b):
                    pool.wait_ge(landed[b].sem, data(landed[b], g, b, loads))
                    nc.gpsimd.tensor_tensor(out=v3(A, b), in0=v3(A, b), in1=per_feature(bias), op=ALU.add
                                            ).then_inc(shifted.sem, 1)

                def average(g, b):
                    hold(pool, landed[b].sem, data(landed[b], g, b, loads), self.turns)
                    cols = bass.ds(g * J, J) if not isinstance(g, int) else slice(g * J, (g + 1) * J)
                    nc.gpsimd.tensor_tensor(out=v3(X, b), in0=v3(X, b),
                                            in1=dinv[:, cols].unsqueeze(2).to_broadcast([NP_, J, D]), op=ALU.mult
                                            ).then_inc(averaged.sem, 1)

                def add_x3(g, b):
                    pool.wait_ge(active.sem, active.at + g + 1)
                    hold(pool, x3_there[b].sem, data(x3_there[b], g, b), self.turns)
                    nc.gpsimd.tensor_tensor(out=v2(Rr, b), in0=v2(Rr, b), in1=v2(X3, b), op=ALU.add
                                            ).then_inc(added.sem, 1)

                def centre(g, b):
                    hold(pool, stored[b].sem, before(stored[b], g, b), self.turns)
                    if kind == "d2":
                        hold(pool, copied.sem, copied.at + g * 2 + 2, self.turns)
                    pool.wait_ge(summed.sem, summed.at + g + 1)
                    nc.gpsimd.tensor_tensor(out=v3(C, b), in0=v3(Rr, b), in1=per_row(mean, b), op=ALU.add
                                            ).then_inc(centred.sem, 1)

                def divide(g, b):
                    pool.wait_ge(inverted.sem, inverted.at + g + 1 + B)
                    nc.gpsimd.tensor_tensor(out=v3(C, b), in0=v3(C, b), in1=per_row(inv, b), op=ALU.mult
                                            ).then_inc(divided.sem, 1)
                parts = [(6 + late, divide), (4 + late, centre)] if normed else []
                if kind == "d4":
                    parts.append((4, add_x3))
                if kind == "d3":
                    parts.append((2, average))
                if conv:
                    parts.append((2, shift))
                run(pool, parts)
        n_src = 2 if kind == "d0" else 1
        read.at += NG + B
        const.at += 2
        wts.at += 16 * n_w
        keys.at += 16 * NG * (brow is not None)
        inner.at += NG * {"d0": 3, "d1": 2, "d2": 2, "d3": 2, "d4": 2}[kind]
        totalled.at += NG * (kind == "d4")
        spread.at += B + NG * normed
        rooted.at += B + NG * normed
        inverted.at += B + NG * normed
        copied.at += 2 * B + (2 * n_src * NG if mm_from is not None else 0)
        kept.at += 4 + 2 * NG * (product_to is not None)
        for sg in (summed, squared):
            sg.at += NG * normed
        for sg in (centred, divided):
            sg.at += (NG + B) * normed
        if mm_from is not None:
            turned.at += 2 * n_src * NG
            product.at += NG + 2
        shifted.at += NG * conv
        active.at += NG * conv
        averaged.at += NG * conv
        added.at += (NG + B) * (kind == "d4")
        scaled.at += NG * (kind == "d1")
        for b in range(B):
            groups = 16 * len(range(b, NG, B))
            landed[b].at += groups * loads
            x3_there[b].at += groups * (kind == "d4")
            stored[b].at += groups * normed
            zstored[b].at += groups * (product_to is not None)


def build_program(nc, x, src, dst, edge_attr_17, W1, b1, W2, b2, Ws, bs, Wn, bn, V1, c1, V2, c2, prelu_a, out):
    ins = dict(x=x, src=src, dst=dst, ea=edge_attr_17, W1=W1, b1=b1, W2=W2, b2=b2, Ws=Ws, bs=bs, Wn=Wn, bn=bn,
               V1=V1, c1=c1, V2=V2, c2=c2, prelu_a=prelu_a)
    with ExitStack() as ctx:
        Program(nc, ctx, ins, out).build()


_INS = ['x', 'src', 'dst', 'edge_attr_17', 'L0_gnn_W1', 'L0_gnn_b1', 'L0_gnn_W2', 'L0_gnn_b2', 'L0_gnn_Ws', 'L0_gnn_bs',
        'L0_gnn_Wn', 'L0_gnn_bn', 'L3_gnn_W1', 'L3_gnn_b1', 'L3_gnn_W2', 'L3_gnn_b2', 'L3_gnn_prelu_a']
_OUTS = [((N, D), 'float32')]


def kernel(**inputs):
    import numpy as _np
    import concourse.bacc as _bacc
    from concourse import mybir as _mybir
    from concourse.bass_utils import run_bass_kernel_spmd as _run

    nc = _bacc.Bacc("TRN2", target_bir_lowering=False, num_devices=1)
    arrays, args = {}, []
    for name in _INS:
        a = _np.ascontiguousarray(inputs[name])
        arrays[f"in_{name}_dram"] = a
        args.append(nc.dram_tensor(f"in_{name}_dram", a.shape, _mybir.dt.from_np(a.dtype), kind="ExternalInput").ap())
    for i, (shape, dtype) in enumerate(_OUTS):
        dt = _mybir.dt.from_np(_np.dtype(dtype))
        args.append(nc.dram_tensor(f"out_{i}_dram", shape, dt, kind="ExternalOutput").ap())
    build_program(nc, *args)
    r = _run(nc, [arrays], core_ids=[0])
    return r.results[0]["out_0_dram"]
```
